# Optimizing a Trainium2 kernel written in Bass

```python
import numpy as np
import jax
import jax.numpy as jnp

def _softmax(x, axis=-1):
    return jax.nn.softmax(x, axis=axis)

def _gelu(x):
    return jax.nn.gelu(x, approximate=True)

def _silu(x):
    return jax.nn.silu(x)

def _sigmoid(x):
    return jax.nn.sigmoid(x)

def _layernorm(x, axis=-1, eps=1e-05):
    m = jnp.mean(x, axis=axis, keepdims=True)
    v = jnp.var(x, axis=axis, keepdims=True)
    return (x - m) / jnp.sqrt(v + eps)

def _scatter_add(tgt, idx, src, axis=0):
    return tgt.at[idx].add(src)

def _segment_sum(src, seg, n):
    return jax.ops.segment_sum(src, seg, n)
kernel_name = 'mk_rec_standalone_d1_rec_r8_b161b8'

def setup_inputs(seed: int=0):
    np.random.seed(seed)
    _w = jnp.asarray

    def _rec_inputs():
        import jax
        import jax.numpy as jnp
        _rk = jax.random.key(seed)
        r_goby_idx = jax.random.randint(jax.random.fold_in(_rk, 1), (2048,), 0, 100, jnp.int32)
        r_is_indel = jax.random.randint(jax.random.fold_in(_rk, 2), (2048,), 0, 2, jnp.int32)
        r_matches_ref = jax.random.randint(jax.random.fold_in(_rk, 3), (2048,), 0, 2, jnp.int32)
        r_from_seq = jax.random.randint(jax.random.fold_in(_rk, 4), (2048, 64), 0, 85, jnp.int32)
        r_to_seq = jax.random.randint(jax.random.fold_in(_rk, 5), (2048, 64), 0, 85, jnp.int32)
        r_count_fwd = jax.random.randint(jax.random.fold_in(_rk, 6), (2048,), 28, 99994, jnp.int32)
        r_count_rev = jax.random.randint(jax.random.fold_in(_rk, 7), (2048,), 22, 12498, jnp.int32)
        r_nwf_numbers = jax.random.randint(jax.random.fold_in(_rk, 8), (11, 2048, 32), 0, 100, jnp.int32)
        r_nwf_freqs = jax.random.randint(jax.random.fold_in(_rk, 9), (11, 2048, 32), 0, 1000, jnp.int32)
        return (r_goby_idx, r_is_indel, r_matches_ref, r_from_seq, r_to_seq, r_count_fwd, r_count_rev, r_nwf_numbers, r_nwf_freqs)
    r_goby_idx, r_is_indel, r_matches_ref, r_from_seq, r_to_seq, r_count_fwd, r_count_rev, r_nwf_numbers, r_nwf_freqs = _rec_inputs()

    def _L0_rec_setup():
        import jax, jax.numpy as jnp
        import numpy as np
        B = 512
        LS = 64
        LN = 32
        FM = [0, 0, 1, 1, 2, 2, 3, 3, 4, 5, 5]

        def lstm_last(x, Wx, Wh, b):
            Bs, H = (x.shape[0], Wh.shape[0])

            def step(carry, xt):
                h, c = carry
                g = xt @ Wx + h @ Wh + b
                i, f, gg, o = jnp.split(g, 4, axis=-1)
                c = jax.nn.sigmoid(f) * c + jax.nn.sigmoid(i) * jnp.tanh(gg)
                h = jax.nn.sigmoid(o) * jnp.tanh(c)
                return ((h, c), None)
            init = (jnp.zeros((Bs, H), x.dtype), jnp.zeros((Bs, H), x.dtype))
            (h, _), _ = jax.lax.scan(step, init, jnp.swapaxes(x, 0, 1))
            return h
        key = jax.random.key(seed)
        ks = jax.random.split(key, 24)
        s = 0.1
        inp = {}
        inp['goby_idx'] = jax.random.randint(ks[0], (B,), 0, 100)
        inp['is_indel'] = jax.random.randint(ks[1], (B,), 0, 2)
        inp['matches_ref'] = jax.random.randint(ks[2], (B,), 0, 2)
        inp['from_seq'] = jax.random.randint(ks[3], (B, LS), 0, 85)
        inp['to_seq'] = jax.random.randint(ks[4], (B, LS), 0, 85)
        inp['count_fwd'] = jax.random.randint(ks[5], (B,), 0, 12500)
        inp['count_rev'] = jax.random.randint(ks[6], (B,), 0, 12500)
        inp['nwf_numbers'] = jax.random.randint(ks[7], (11, B, LN), 0, 100)
        inp['nwf_freqs'] = jax.random.randint(ks[8], (11, B, LN), 0, 1000)
        inp['goby_emb'] = jax.random.normal(ks[9], (100, 4)) * s
        inp['bool_emb'] = jax.random.normal(ks[10], (2, 2)) * s
        inp['count_emb'] = jax.random.normal(ks[11], (12500, 5)) * s
        inp['base_emb'] = jax.random.normal(ks[12], (85, 6)) * s
        inp['seq_Wx'] = jax.random.normal(ks[13], (6, 256)) * s
        inp['seq_Wh'] = jax.random.normal(ks[14], (64, 256)) * s
        inp['seq_b'] = jnp.zeros((256,))
        inp['nwf_num_emb'] = jax.random.normal(ks[15], (6, 1000, 4)) * s
        inp['nwf_freq_emb'] = jax.random.normal(ks[16], (6, 1000, 4)) * s
        inp['nwf_Wx'] = jax.random.normal(ks[17], (6, 8, 32)) * s
        inp['nwf_Wh'] = jax.random.normal(ks[18], (6, 8, 32)) * s
        inp['nwf_b'] = jnp.zeros((6, 32))
        inp['reduce_W'] = jax.random.normal(ks[19], (234, 64)) * s
        inp['reduce_b'] = jnp.zeros((64,))
        return inp
    _L0_rec_all = _L0_rec_setup()
    _L0_rec_in = {k: v for k, v in _L0_rec_all.items() if k in ('goby_emb', 'bool_emb', 'count_emb', 'base_emb', 'seq_Wx', 'seq_Wh', 'seq_b', 'nwf_num_emb', 'nwf_freq_emb', 'nwf_Wx', 'nwf_Wh', 'nwf_b', 'reduce_W', 'reduce_b')}
    del _L0_rec_all
    return {'r_goby_idx': r_goby_idx, 'r_is_indel': r_is_indel, 'r_matches_ref': r_matches_ref, 'r_from_seq': r_from_seq, 'r_to_seq': r_to_seq, 'r_count_fwd': r_count_fwd, 'r_count_rev': r_count_rev, 'r_nwf_numbers': r_nwf_numbers, 'r_nwf_freqs': r_nwf_freqs, 'L0_rec_goby_emb': _L0_rec_in['goby_emb'], 'L0_rec_bool_emb': _L0_rec_in['bool_emb'], 'L0_rec_count_emb': _L0_rec_in['count_emb'], 'L0_rec_base_emb': _L0_rec_in['base_emb'], 'L0_rec_seq_Wx': _L0_rec_in['seq_Wx'], 'L0_rec_seq_Wh': _L0_rec_in['seq_Wh'], 'L0_rec_seq_b': _L0_rec_in['seq_b'], 'L0_rec_nwf_num_emb': _L0_rec_in['nwf_num_emb'], 'L0_rec_nwf_freq_emb': _L0_rec_in['nwf_freq_emb'], 'L0_rec_nwf_Wx': _L0_rec_in['nwf_Wx'], 'L0_rec_nwf_Wh': _L0_rec_in['nwf_Wh'], 'L0_rec_nwf_b': _L0_rec_in['nwf_b'], 'L0_rec_reduce_W': _L0_rec_in['reduce_W'], 'L0_rec_reduce_b': _L0_rec_in['reduce_b']}

def reference(r_goby_idx, r_is_indel, r_matches_ref, r_from_seq, r_to_seq, r_count_fwd, r_count_rev, r_nwf_numbers, r_nwf_freqs, L0_rec_goby_emb, L0_rec_bool_emb, L0_rec_count_emb, L0_rec_base_emb, L0_rec_seq_Wx, L0_rec_seq_Wh, L0_rec_seq_b, L0_rec_nwf_num_emb, L0_rec_nwf_freq_emb, L0_rec_nwf_Wx, L0_rec_nwf_Wh, L0_rec_nwf_b, L0_rec_reduce_W, L0_rec_reduce_b):
    import jax
    import jax.numpy as jnp

    def _L0_rec_ref(goby_emb, bool_emb, count_emb, base_emb, seq_Wx, seq_Wh, seq_b, nwf_num_emb, nwf_freq_emb, nwf_Wx, nwf_Wh, nwf_b, reduce_W, reduce_b, goby_idx, is_indel, matches_ref, from_seq, to_seq, count_fwd, count_rev, nwf_numbers, nwf_freqs):
        import jax, jax.numpy as jnp
        import numpy as np
        B = 512
        LS = 64
        LN = 32
        FM = [0, 0, 1, 1, 2, 2, 3, 3, 4, 5, 5]

        def lstm_last(x, Wx, Wh, b):
            Bs, H = (x.shape[0], Wh.shape[0])

            def step(carry, xt):
                h, c = carry
                g = xt @ Wx + h @ Wh + b
                i, f, gg, o = jnp.split(g, 4, axis=-1)
                c = jax.nn.sigmoid(f) * c + jax.nn.sigmoid(i) * jnp.tanh(gg)
                h = jax.nn.sigmoid(o) * jnp.tanh(c)
                return ((h, c), None)
            init = (jnp.zeros((Bs, H), x.dtype), jnp.zeros((Bs, H), x.dtype))
            (h, _), _ = jax.lax.scan(step, init, jnp.swapaxes(x, 0, 1))
            return h
        fm = jnp.array(FM)
        m_from = lstm_last(base_emb[from_seq], seq_Wx, seq_Wh, seq_b)
        m_to = lstm_last(base_emb[to_seq], seq_Wx, seq_Wh, seq_b)

        def enc(ne, fe, Wx, Wh, b, nums, fr):
            x = jnp.concatenate([ne[nums], fe[fr]], axis=-1)
            return lstm_last(x, Wx, Wh, b)
        nwf = jax.vmap(enc)(nwf_num_emb[fm], nwf_freq_emb[fm], nwf_Wx[fm], nwf_Wh[fm], nwf_b[fm], nwf_numbers, nwf_freqs)
        nwf = jnp.swapaxes(nwf, 0, 1).reshape(goby_idx.shape[0], 11 * 8)
        feats = jnp.concatenate([goby_emb[goby_idx], bool_emb[is_indel], bool_emb[matches_ref], m_from, m_to, count_emb[count_fwd], count_emb[count_rev], nwf], axis=-1)
        return jax.nn.relu(feats @ reduce_W + reduce_b)
    y = _L0_rec_ref(L0_rec_goby_emb, L0_rec_bool_emb, L0_rec_count_emb, L0_rec_base_emb, L0_rec_seq_Wx, L0_rec_seq_Wh, L0_rec_seq_b, L0_rec_nwf_num_emb, L0_rec_nwf_freq_emb, L0_rec_nwf_Wx, L0_rec_nwf_Wh, L0_rec_nwf_b, L0_rec_reduce_W, L0_rec_reduce_b, r_goby_idx, r_is_indel, r_matches_ref, r_from_seq, r_to_seq, r_count_fwd, r_count_rev, r_nwf_numbers, r_nwf_freqs)
    return y

_drawn_inputs = setup_inputs


def setup_inputs(seed=0):
    import zlib

    import numpy as np

    out = dict(_drawn_inputs(seed))
    spreads = {'L0_rec_seq_b': (0.0, 0.1), 'L0_rec_nwf_b': (0.0, 0.1), 'L0_rec_reduce_b': (0.0, 0.1)}
    factors = {}
    for name, (base, spread) in spreads.items():
        noise = np.random.default_rng([zlib.crc32(name.encode()), seed]).standard_normal(out[name].shape)
        drawn = base * np.exp(spread * noise) if base else spread * noise
        out[name] = jnp.asarray(drawn.astype(out[name].dtype))
    for name, factor in factors.items():
        out[name] = (out[name] * factor).astype(out[name].dtype)
    return out
```

```python
from contextlib import ExitStack

import numpy as np
import concourse.bass as bass
from concourse import mybir

F32 = mybir.dt.float32
BF16 = mybir.dt.bfloat16
I32 = mybir.dt.int32
ALU = mybir.AluOpType
ACT = mybir.ActivationFunctionType

P = 128
B = 2048
SLOTS = B // P
LANES = P
SEQ_T, NWF_T = 64, 32
SEQ_H, SEQ_E, VOCAB = 64, 6, 85
NWF_H, NWF_E, NWF_ROWS = 8, 8, 1000
FEATURES = 11
SETS = [(0, 2), (2, 2), (4, 2), (6, 2), (8, 1), (9, 2)]
NSETS = len(SETS)
OUT = 64
GATES = [(0, ACT.Sigmoid), (2, ACT.Tanh), (1, ACT.Sigmoid), (3, ACT.Sigmoid)]
CH = 512

CELLS = [("seq", 0, 0), ("seq", 0, 1), ("seq", 0, 2), ("nwf", None, 0), ("seq", 0, 3), ("seq", 1, 0),
         ("seq", 1, 1), ("nwf", None, 1), ("seq", 1, 2), ("seq", 1, 3), ("nwf", None, 2)]
NC = len(CELLS)
NWF_CELLS = [(0, 512), (512, 512), (1024, 384)]

UNITS = []
for _m, (_f, _n) in enumerate(SETS):
    for _ty in range(2):
        for _q in ([(0, 1), (2, 3)] if _n == 2 else [(0, 1, 2, 3)]):
            UNITS.append((_ty, _m, _q))
NU = len(UNITS)
NS = 8
STORED_AS = [FEATURES * ty + 2 * m - (m == 5) + (q[0] // 2) for ty, m, q in UNITS]
SET_END = [max(u for u, x in enumerate(UNITS) if x[1] == m) for m in range(NSETS)]
SET_SLOT = [e // 2 + 1 for e in SET_END]
QUAD_AT = [64, 96, 0, 32]
RING = 4

C_ID, C_RED, C_LOW, C_HIGH, C_ALL = 0, 128, 192, 193, 194


class Round:

    def __init__(self, i, times, plus):
        self.i, self.times, self.plus = i, times, plus

    def count(self, each, more, per=1):
        if self.i is None:
            return (each * self.plus + more) // per
        return self.i * (self.times * each // per) + (each * self.plus + more) // per

    @property
    def parity(self):
        return self.plus % 2


def at_least(eng, sem, value):
    if isinstance(value, int) and value <= 0:
        return
    eng.wait_ge(sem, value)


def unit_of(r, u):
    return (NU * r.plus + u) % RING


def build(nc, goby_idx, is_indel, matches_ref, from_seq, to_seq, count_fwd, count_rev, numbers, freqs,
          goby_emb, bool_emb, count_emb, base_emb, seq_Wx, seq_Wh, seq_b, num_emb, freq_emb,
          nwf_Wx, nwf_Wh, nwf_b, reduce_W, reduce_b, consts, out):
    ctx = ExitStack()
    with ctx:
        def sb(name, shape, dt, stack=ctx):
            return stack.enter_context(nc.sbuf_tensor(name, shape, dt))

        def sem(name):
            return ctx.enter_context(nc.semaphore(name))

        low_dram = nc.dram_tensor("low_digits", [NWF_T, NU, 4, CH], BF16, kind="Internal").ap()
        high_dram = nc.dram_tensor("high_digits", [NWF_T, NU, 4, CH], BF16, kind="Internal").ap()
        tok_dram = nc.dram_tensor("seq_tokens", [SEQ_T, SLOTS // 2, 2, 2, LANES], BF16, kind="Internal").ap()

        cst = sb("cst", [P, C_ALL], F32)
        seq_hx = [[sb(f"seq_hx{p}{z}", [P, B], F32) for z in range(2)] for p in range(2)]
        seq_c = sb("seq_c", [P, B], F32)
        nwf_hx = [[sb(f"nwf_hx{p}{z}", [P, FEATURES * LANES], F32) for z in range(2)] for p in range(2)]
        nwf_c = sb("nwf_c", [P, FEATURES * LANES], F32)
        seq_w = sb("seq_w", [P, 2, 4, SEQ_H], F32)
        nwf_w = sb("nwf_w", [P, 2, NSETS, 4, 64], F32)
        nwf_bias = sb("nwf_bias", [P, NSETS, 4], F32)
        tab = sb("tab", [P, 3, 2 * NSETS, 32], BF16)
        seq_tab = sb("seq_tab", [P, 3, 32], BF16)
        small = sb("small", [P, 4 * LANES], F32)
        small_w = sb("small_w", [P, 4, OUT], F32)

        prep = ExitStack()
        idx_in = sb("idx_in", [P, FEATURES, SLOTS * NWF_T], I32, prep)
        idx_f = sb("idx_f", [P, FEATURES, SLOTS * NWF_T], F32, prep)
        dig_i = sb("dig_i", [P, FEATURES, SLOTS * NWF_T], I32, prep)
        dig = sb("dig", [P, FEATURES, SLOTS * NWF_T], BF16, prep)
        turned = sb("turned", [P, FEATURES, 4, LANES], BF16, prep)
        ident_bf = sb("ident_bf", [P, P], BF16, prep)
        tab_f = sb("tab_f", [P, 2 * NSETS + 1, 8, 4], F32, prep)
        tab_r = sb("tab_r", [P, 2 * NSETS + 1, 8, 4], F32, prep)
        few_in = sb("few_in", [P, 5, SLOTS], I32, prep)
        few_f = sb("few_f", [P, 5, SLOTS], F32, prep)
        few_idx = sb("few_idx", [P, 5, SLOTS], I32, prep)
        small_rows = sb("small_rows", [P, SLOTS, 32], F32, prep)
        tp = [prep.enter_context(nc.psum_tensor(f"tp{n}", [P, 4, LANES], BF16)) for n in range(2)]
        tps = prep.enter_context(nc.psum_tensor("tps", [P, 4 * LANES], F32))

        s_cst = sem("s_cst")
        s_idx = sem("s_idx")
        s_zero = sem("s_zero")
        s_weights = sem("s_weights")
        s_tables = sem("s_tables")
        s_few = sem("s_few")
        s_gather = sem("s_gather")
        s_few_idx = sem("s_few_idx")
        s_small_zero = sem("s_small_zero")
        s_digits = sem("s_digits")
        s_turned = sem("s_turned")
        s_out_of_psum = sem("s_out_of_psum")
        s_stored = sem("s_stored")
        s_chain = sem("s_chain")
        s_small_t = sem("s_small_t")

        nwf_idx = [numbers, freqs]
        seq_idx = [from_seq, to_seq]
        PASSES = [(0, "low"), (0, "high"), (1, "low"), (1, "high"), (2, "seq"), (3, "seq")]
        NBLK = [FEATURES * 4] * 4 + [8] * 2

        def idx_view(k):
            if k < 2:
                return idx_in[:, :, :], nwf_idx[k].rearrange("j (b s) t -> b j (s t)", s=SLOTS)
            return (idx_in[:, 0:2, :].rearrange("p j c -> p (j c)"),
                    seq_idx[k - 2].rearrange("(b s) t -> b (s t)", s=SLOTS))

        def groups(n):
            return NBLK[n] // 4

        done_before = [sum(groups(m) for m in range(n)) for n in range(len(PASSES) + 1)]
        STORES = [4] * 4 + [2] * 2
        stored_before = [sum(STORES[:n]) for n in range(len(PASSES) + 1)]
        n_gather = 5 * SLOTS

        with nc.Block() as block:
            weight_dmas = []
            for z in range(2):
                hrow, xrow = (0, 64) if z == 0 else (64, 0)
                for n, (g, _) in enumerate(GATES):
                    cols = slice(g * SEQ_H, (g + 1) * SEQ_H)
                    weight_dmas.append((seq_w[hrow:hrow + SEQ_H, z, n, :], seq_Wh[:, cols]))
                    weight_dmas.append((seq_w[xrow:xrow + SEQ_E, z, n, :], seq_Wx[:, cols]))
                    weight_dmas.append((seq_w[xrow + SEQ_E:xrow + SEQ_E + 1, z, n, :], seq_b[None, cols]))
            for z in range(2):
                for s in range(8):
                    for n, (g, _) in enumerate(GATES):
                        for base, w in ((64 * z, nwf_Wh), (64 - 64 * z, nwf_Wx)):
                            weight_dmas.append((nwf_w[base + 8 * s:base + 8 * s + 8, z, :, n, 8 * s:8 * s + 8],
                                                w.rearrange("m d (g u) -> d m g u", g=4)[:, :, g, :]))
            bias_rows = nwf_b.rearrange("m (g u) -> u m g", g=4)
            for r in range(4):
                weight_dmas.append((small_w[32 * r:32 * r + 8, r, :], reduce_W[0:8, :]))
                weight_dmas.append((small_w[32 * r + 8:32 * r + 18, r, :], reduce_W[136:146, :]))
                weight_dmas.append((small_w[32 * r + 18:32 * r + 19, r, :], reduce_b[None, :]))
            NW = len(weight_dmas)
            table_dmas = []
            for ty, src in enumerate((num_emb, freq_emb)):
                for m in range(NSETS):
                    table_dmas.append((tab_f[:, 2 * m + ty, 0:7, :],
                                       src[m, 0:7 * P, :].rearrange("(a b) d -> b a d", b=P)))
                    table_dmas.append((tab_f[0:NWF_ROWS - 7 * P, 2 * m + ty, 7, :], src[m, 7 * P:NWF_ROWS, :]))
            table_dmas.append((tab_f[0:VOCAB, 2 * NSETS, :, :].rearrange("p a d -> p (a d)")[:, 0:SEQ_E], base_emb))
            NT = len(table_dmas)

            def store_digits(sp, dram, ty, done):
                for r in range(4):
                    rows = turned[32 * r:32 * r + 32, :, :, :].rearrange("p j q l -> p (j q l)")
                    sp.dma_start(dram[:, FEATURES * ty:FEATURES * (ty + 1), r, :],
                                 rows.rearrange("p (u c) -> p u c", c=CH)).then_inc(done, 16)

            def store_tokens(sp, z, done):
                flat = turned[:, :, :, :].rearrange("p j q l -> p (j q l)")
                for odd in range(2):
                    sp.dma_start(tok_dram[:, :, z, odd, :],
                                 flat[64 * odd:64 * odd + 64, 0:8 * LANES]
                                 .rearrange("p (h l) -> p h l", h=8)).then_inc(done, 16)

            def turned_at(j):
                flat = turned[:, :, :, :].rearrange("p j q l -> p (j q l)")
                if j == 8:
                    return flat[:, 8 * CH:9 * CH].rearrange("p (q l) -> p q l", q=4)
                m, i = (j // 2, j % 2) if j < 8 else (4, j - 9)
                at = m * 2 * CH if j < 8 else 9 * CH
                return flat[:, at:at + 2 * CH].rearrange("p (q i l) -> p q i l", q=4, i=2)[:, :, i, :]

            @block.sync
            def _(sp):
                sp.dma_start(cst[:, :], consts).then_inc(s_cst, 16)
                for n, (k, kind) in enumerate(PASSES):
                    if kind != "high":
                        if n > 0:
                            sp.wait_ge(s_digits, n)
                        dst, src = idx_view(k)
                        sp.dma_start(dst, src).then_inc(s_idx, 16)
                    if n == 0:
                        sp.wait_ge(s_zero, 1)
                        for dst, src in weight_dmas[:NW // 2]:
                            sp.dma_start(dst, src).then_inc(s_weights, 16)
                    sp.wait_ge(s_out_of_psum, done_before[n + 1])
                    if k < 2:
                        dram = low_dram if kind == "low" else high_dram
                        store_digits(sp, dram, k, s_stored)
                    else:
                        store_tokens(sp, k - 2, s_stored)
                sp.wait_ge(s_stored, 16 * stored_before[-1])

            @block.scalar
            def _(act):
                for n, src in enumerate((goby_idx, is_indel, matches_ref, count_fwd, count_rev)):
                    act.dma_start(few_in[:, n, :], src.rearrange("(b s) -> b s", s=SLOTS)).then_inc(s_few, 16)
                for s in range(SLOTS):
                    act.dma_start(nwf_bias[8 * s:8 * s + 8, :, :], bias_rows,
                                  allow_slow_non_contiguous=True).then_inc(s_weights, 16)
                act.wait_ge(s_zero, 1)
                for dst, src in table_dmas:
                    act.dma_start(dst, src).then_inc(s_tables, 16)
                for dst, src in weight_dmas[NW // 2:]:
                    act.dma_start(dst, src).then_inc(s_weights, 16)
                done = 0
                for n in range(len(PASSES)):
                    if n > 0:
                        act.wait_ge(s_stored, 16 * stored_before[n])
                    for grp in range(groups(n)):
                        act.wait_ge(s_turned, done + 1)
                        if n < 4:
                            dst = turned_at(grp)
                        else:
                            dst = turned[:, grp, :, :]
                        nc.scalar.copy(dst, tp[done % 2][:, :, :]).then_inc(s_out_of_psum, 1)
                        done += 1
                act.wait_ge(s_small_t, 1)
                nc.scalar.copy(small[:, :], tps[:, :]).then_inc(s_out_of_psum, 1)
                act.wait_ge(s_weights, 16 * (NW + SLOTS))

            @block.gpsimd
            def _(pool):
                nc.gpsimd.memset(small_rows[:, :, :], 0.0).then_inc(s_small_zero, 1)
                pool.wait_ge(s_small_zero, 1)
                nc.gpsimd.memset(small_rows[:, :, 18:19], 1.0).then_inc(s_small_zero, 1)
                pool.wait_ge(s_few_idx, 1)
                at = 0
                for n, (table, width) in enumerate(((goby_emb, 4), (bool_emb, 2), (bool_emb, 2), (count_emb, 5),
                                                    (count_emb, 5))):
                    for s in range(SLOTS):
                        nc.gpsimd.indirect_dma_start(
                            out=small_rows[:, s, at:at + width], out_offset=None, in_=table,
                            in_offset=bass.IndirectOffsetOnAxis(ap=few_idx[:, n, s:s + 1], axis=0)
                        ).then_inc(s_gather, 16)
                    at += width

            @block.vector
            def _(dve):
                chain = [0]

                def link(ins):
                    chain[0] += 1
                    ins.then_inc(s_chain, 1)
                    dve.wait_ge(s_chain, chain[0])

                nc.vector.memset(seq_w[:, :, :, :], 0.0)
                nc.vector.memset(nwf_w[:, :, :, :, :], 0.0)
                nc.vector.memset(small_w[:, :, :], 0.0)
                nc.vector.memset(tab_f[:, :, :, :], 0.0).then_inc(s_zero, 1)
                dve.wait_ge(s_cst, 16)
                nc.vector.tensor_copy(ident_bf[:, :], cst[:, C_ID:C_ID + P])

                def in_range(dst, src, rows):
                    link(nc.vector.tensor_scalar(dst, src, 0.0, float(rows), ALU.is_lt, ALU.mult))
                    link(nc.vector.tensor_tensor(dst, dst, src, ALU.add))
                    link(nc.vector.tensor_scalar(dst, dst, 0.0, float(rows - 1), ALU.max, ALU.min))

                dve.wait_ge(s_few, 16 * 5)
                for n, rows in enumerate((100, 2, 2, 12500, 12500)):
                    in_range(few_f[:, n, :], few_in[:, n, :], rows)
                nc.vector.tensor_copy(few_idx[:, :, :], few_f[:, :, :]).then_inc(s_few_idx, 1)

                for n, (k, kind) in enumerate(PASSES):
                    if kind != "high":
                        dve.wait_ge(s_idx, 16 * (sum(x != "high" for _, x in PASSES[:n]) + 1))
                        rows = NWF_ROWS if k < 2 else VOCAB
                        w = FEATURES * SLOTS * NWF_T if k < 2 else SLOTS * SEQ_T
                        src = idx_in[:, :, :].rearrange("p j c -> p (j c)")[:, 0:w]
                        val = idx_f[:, :, :].rearrange("p j c -> p (j c)")[:, 0:w]
                        whole = dig_i[:, :, :].rearrange("p j c -> p (j c)")[:, 0:w]
                        d = dig[:, :, :].rearrange("p j c -> p (j c)")[:, 0:w]
                        in_range(val, src, rows)
                    if n > 0:
                        dve.wait_ge(s_turned, done_before[n])
                    if kind == "seq":
                        nc.vector.tensor_copy(d, val).then_inc(s_digits, 1)
                        continue
                    link(nc.vector.tensor_copy(whole, val))
                    link(nc.vector.tensor_scalar(whole, whole, 127 if kind == "low" else 896, None, ALU.bitwise_and))
                    nc.vector.tensor_copy(d, whole).then_inc(s_digits, 1)
                for p in range(2):
                    for z in range(2):
                        nc.vector.memset(seq_hx[p][z][:, :], 0.0)
                        nc.vector.memset(nwf_hx[p][z][:, :], 0.0)
                nc.vector.memset(seq_c[:, :], 0.0)
                nc.vector.memset(nwf_c[:, :], 0.0)
                dve.wait_ge(s_tables, 16 * NT)
                link(nc.vector.memset(tab_f[:, 2 * NSETS, 1, 2:3], 1.0))
                left = tab_f[:, :, :, :].rearrange("p n a d -> p n (a d)")
                rest = tab_r[:, :, :, :].rearrange("p n a d -> p n (a d)")
                for part in range(3):
                    for dst, rows in ((tab[:, part, :, :], slice(0, 2 * NSETS)),
                                      (seq_tab[:, part:part + 1, :], slice(2 * NSETS, 2 * NSETS + 1))):
                        link(nc.vector.tensor_copy(dst, left[:, rows, :]))
                        if part < 2:
                            link(nc.vector.tensor_tensor(rest[:, rows, :], left[:, rows, :], dst, ALU.subtract))
                    left, rest = rest, left

            @block.tensor
            def _(pe):
                done = 0
                for n in range(len(PASSES)):
                    pe.wait_ge(s_digits, n + 1)
                    flat = dig[:, :, :].rearrange("p j c -> p (j c)")
                    for grp in range(groups(n)):
                        if done >= 2:
                            pe.wait_ge(s_out_of_psum, done - 1)
                        for q in range(4):
                            last = nc.tensor.transpose(tp[done % 2][:, q, :],
                                                       flat[:, (4 * grp + q) * P:(4 * grp + q + 1) * P], ident_bf[:, :])
                        last.then_inc(s_turned, 1)
                        done += 1
                pe.wait_ge(s_cst, 16)
                pe.wait_ge(s_small_zero, 2)
                pe.wait_ge(s_gather, 16 * n_gather)
                rows = small_rows[:, :, :].rearrange("b s d -> b (s d)")
                for q in range(4):
                    last = nc.tensor.transpose(tps[:, q * LANES:(q + 1) * LANES], rows[:, q * P:(q + 1) * P],
                                               cst[:, C_ID:C_ID + P])
                last.then_inc(s_small_t, 1)

        prep.close()

        work = ExitStack()
        low = sb("low", [P, RING, 4 * CH], BF16, work)
        high = sb("high", [P, RING, CH], BF16, work)
        onehot = sb("onehot", [P, RING, 4 * CH], BF16, work)
        kept = sb("kept", [P, RING, CH], F32, work)
        tok = sb("tok", [P, RING, 2 * CH], BF16, work)
        seq_onehot = sb("seq_onehot", [P, RING, 2 * CH], BF16, work)
        gates = [[sb(f"gate{g}{p}", [P, CH], F32, work) for p in range(2)] for g in range(4)]
        ig = sb("ig", [P, 2, CH], F32, work)
        tanh_c = sb("tanh_c", [P, 2, CH], F32, work)

        g_ps = [work.enter_context(nc.psum_tensor(f"g_ps{g}", [P, CH], F32)) for g in range(4)]
        e_ps = [work.enter_context(nc.psum_tensor(f"e_ps{n}", [P, CH], F32)) for n in range(2)]
        x_ps = work.enter_context(nc.psum_tensor("x_ps", [P, CH], F32))
        sx_ps = work.enter_context(nc.psum_tensor("sx_ps", [P, CH], F32))

        digits_here = [sem(f"digits_here{n}") for n in range(RING)]
        tokens_here = [sem(f"tokens_here{n}") for n in range(RING)]
        onehot_ready = sem("onehot_ready")
        seq_onehot_ready = sem("seq_onehot_ready")
        looked_up = sem("looked_up")
        kept_ready = sem("kept_ready")
        kept_used = sem("kept_used")
        nwf_x_done = sem("nwf_x_done")
        seq_x_ready = sem("seq_x_ready")
        seq_x_done = sem("seq_x_done")
        gate_ready = sem("gate_ready")
        gate_done = sem("gate_done")
        ig_ready = sem("ig_ready")
        c_scaled = sem("c_scaled")
        c_ready = sem("c_ready")
        tanh_ready = sem("tanh_ready")
        h_low = sem("h_low")
        h_high = sem("h_high")

        def cell_number(r, k, more=0):
            return r.count(NC, k + more + 1 - NC)

        def units(r, u, more=0):
            return r.count(NU, u + 1 + more)

        def sets(r, m, more=0):
            return r.count(NSETS, m + 1 + more)

        def seqs(r, q, more=0):
            return r.count(NS, q + 1 + more)

        def before(r):
            return Round(r.i, r.times, r.plus - 1)

        def cell_cols(cell):
            kind, _, c = cell
            return (c * CH, CH) if kind == "seq" else NWF_CELLS[c]

        def cell_sets(c):
            return [m for m, (f, n) in enumerate(SETS) if NWF_CELLS[c][0] <= f * LANES < sum(NWF_CELLS[c])]

        SEQ_SLOTS = [k for k, cell in enumerate(CELLS) if cell[0] == "seq"]

        def previous_seq(k):
            _, p, c = CELLS[k]
            return (1 - p, next(n for n, x in enumerate(CELLS) if x == ("seq", 1 - p, c)))


        def round_sync(sp, r, step, seq_step):
            for k in range(NC):
                if k in SEQ_SLOTS:
                    q = SEQ_SLOTS.index(k)
                    _, par, c = CELLS[k]
                    at = (NS * r.plus + q) % RING
                    at_least(sp, seq_onehot_ready, seqs(r, q, -RING))
                    sp.dma_start(tok[:, at, :],
                                 tok_dram[bass.ds(seq_step + par, 1), 2 * c:2 * c + 2, :, :, :]
                                 .rearrange("t h z o l -> t (h z o l)")
                                 .to_broadcast([P, 2 * CH])).then_inc(tokens_here[at], 16)
                for u in (2 * k, 2 * k + 1):
                    at = unit_of(r, u)
                    at_least(sp, kept_ready, units(r, u, -RING))
                    sp.dma_start(low[:, at, :],
                                 low_dram[bass.ds(step, 1), STORED_AS[u], :, :].rearrange("t r c -> t (r c)")
                                 .to_broadcast([P, 4 * CH])).then_inc(digits_here[at], 16)
                    for g in range(4):
                        sp.dma_start(high[32 * g:32 * g + 32, at, :],
                                     high_dram[bass.ds(step, 1), STORED_AS[u], g, :]
                                     .to_broadcast([32, CH])).then_inc(digits_here[at], 16)

        def keep_wanted(dve, r, u):
            at = unit_of(r, u)
            at_least(dve, looked_up, units(r, u))
            at_least(dve, kept_used, units(r, u, -RING))
            nc.vector.scalar_tensor_tensor(out=kept[:, at, :], in0=high[:, at, :], scalar=cst[:, C_HIGH:C_HIGH + 1],
                                           in1=e_ps[u % 2][:, :], op0=ALU.is_equal,
                                           op1=ALU.mult).then_inc(kept_ready, 1)

        def new_h(k, r):
            kind, par, c = CELLS[k]
            at, n = cell_cols(CELLS[k])
            if kind == "seq":
                return seq_hx[1 - par][0][0:64, at:at + n], seq_hx[1 - par][1][64:128, at:at + n]
            return nwf_hx[r.parity][0][0:64, at:at + n], nwf_hx[r.parity][1][64:128, at:at + n]

        def new_h_low(pool, r, k, slot2):
            _, n = cell_cols(CELLS[k])
            at_least(pool, tanh_ready, cell_number(r, k))
            nc.gpsimd.tensor_tensor(new_h(k, r)[0], gates[3][slot2][0:64, 0:n], tanh_c[0:64, slot2, 0:n],
                                    ALU.mult).then_inc(h_low, 1)

        def new_h_high(dve, r, k, slot2):
            _, n = cell_cols(CELLS[k])
            at_least(dve, tanh_ready, cell_number(r, k))
            nc.vector.tensor_tensor(new_h(k, r)[1], gates[3][slot2][64:128, 0:n], tanh_c[64:128, slot2, 0:n],
                                    ALU.mult).then_inc(h_high, 1)

        def c_of(k):
            at, n = cell_cols(CELLS[k])
            return (seq_c if CELLS[k][0] == "seq" else nwf_c)[:, at:at + n], n

        def parity2(r, k):
            return (NC * (r.plus - 1) + k) % 2

        def cell_before(r, k):
            return (r, k - 1) if k else (before(r), NC - 1)

        def round_vector(dve, r, cells, lookups, first):
            for k in range(NC):
                if k in SEQ_SLOTS and lookups:
                    q = SEQ_SLOTS.index(k)
                    at = (NS * r.plus + q) % RING
                    at_least(dve, tokens_here[at], seq_fills(r, q))
                    at_least(dve, seq_x_ready, seqs(r, q, -RING))
                    nc.vector.tensor_scalar(seq_onehot[:, at, :], tok[:, at, :], cst[:, C_LOW:C_LOW + 1], None,
                                            ALU.is_equal).then_inc(seq_onehot_ready, 1)
                if k > 0 and lookups:
                    keep_wanted(dve, r, 2 * k - 2)
                    keep_wanted(dve, r, 2 * k - 1)
                if k == 0 and cells:
                    keep_wanted(dve, before(r), NU - 2)
                    keep_wanted(dve, before(r), NU - 1)
                if lookups:
                    for u in (2 * k, 2 * k + 1):
                        at = unit_of(r, u)
                        at_least(dve, digits_here[at], unit_fills(r, u))
                        at_least(dve, looked_up, units(r, u, -RING))
                        nc.vector.tensor_scalar(onehot[:, at, :], low[:, at, :], cst[:, C_LOW:C_LOW + 1], None,
                                                ALU.is_equal).then_inc(onehot_ready, 1)
                if cells:
                    two = parity2(r, k)
                    c, n = c_of(k)
                    at_least(dve, gate_done, r.count(4 * NC, 4 * (k - NC) + 3))
                    nc.vector.tensor_tensor(c, c, gates[2][two][:, 0:n], ALU.mult).then_inc(c_scaled, 1)
                    if not (first and k == 0):
                        new_h_high(dve, *cell_before(r, k), 1 - two)
                    at_least(dve, c_scaled, cell_number(r, k))
                    at_least(dve, ig_ready, cell_number(r, k))
                    nc.vector.tensor_tensor(c, c, ig[:, two, 0:n], ALU.add).then_inc(c_ready, 1)

        def seq_fills(r, q):
            return r.count(16 * NS, 16 * (q // RING) * RING + 16 * RING, RING)

        def unit_fills(r, u):
            return 80 * ((NU * r.plus + u) // RING + 1) + (0 if r.i is None else r.i * (80 * r.times * NU // RING))

        def round_gpsimd(pool, r, first):
            for k in range(NC):
                two = parity2(r, k)
                _, n = cell_cols(CELLS[k])
                at_least(pool, gate_done, r.count(4 * NC, 4 * (k - NC) + 2))
                at_least(pool, c_ready, cell_number(r, k, -2))
                nc.gpsimd.tensor_tensor(ig[:, two, 0:n], gates[0][two][:, 0:n], gates[1][two][:, 0:n],
                                        ALU.mult).then_inc(ig_ready, 1)
                if not (first and k == 0):
                    new_h_low(pool, *cell_before(r, k), 1 - two)

        def tanh_of(act, r, k, slot2):
            c, n = c_of(k)
            at_least(act, c_ready, cell_number(r, k))
            nc.scalar.activation(tanh_c[:, slot2, 0:n], c, ACT.Tanh).then_inc(tanh_ready, 1)

        def store_x(act, r, m):
            f, count = SETS[m]
            at, n = f * LANES, count * LANES
            at_least(act, kept_used, units(r, SET_END[m]))
            hx = nwf_hx[r.parity]
            nc.scalar.copy(hx[0][64:128, at:at + n], x_ps[64:128, 0:n])
            nc.scalar.copy(hx[1][0:64, at:at + n], x_ps[0:64, 0:n]).then_inc(nwf_x_done, 1)

        def round_scalar(act, r, cells, lookups, first):
            for k in range(NC):
                kind, par, c = CELLS[k]
                if cells:
                    two = parity2(r, k)
                    at_least(act, h_low, cell_number(r, k, -2))
                    at_least(act, h_high, cell_number(r, k, -2))
                    at, n = cell_cols(CELLS[k])
                    for g, (place, func) in enumerate(GATES):
                        at_least(act, gate_ready, r.count(4 * NC, 4 * (k - NC) + g + 1))
                        if kind == "seq":
                            last = nc.scalar.activation(gates[g][two][:, :], g_ps[g][:, :], func)
                        else:
                            for m in cell_sets(c):
                                a, w = SETS[m][0] * LANES - at, SETS[m][1] * LANES
                                last = nc.scalar.activation(gates[g][two][:, a:a + w], g_ps[g][:, a:a + w], func,
                                                            bias=nwf_bias[:, m, place:place + 1])
                        last.then_inc(gate_done, 1)
                    if not (first and k == 0):
                        tanh_of(act, *cell_before(r, k), 1 - two)
                if k in SEQ_SLOTS and lookups:
                    q = SEQ_SLOTS.index(k)
                    at_least(act, seq_x_ready, seqs(r, q))
                    nc.scalar.copy(seq_hx[par][0][64:96, c * CH:(c + 1) * CH], sx_ps[64:96, :])
                    nc.scalar.copy(seq_hx[par][1][0:32, c * CH:(c + 1) * CH], sx_ps[0:32, :]).then_inc(seq_x_done, 1)
                for m in range(NSETS):
                    if lookups and SET_SLOT[m] == k:
                        store_x(act, r, m)
                    if cells and SET_SLOT[m] - NC == k:
                        store_x(act, before(r), m)

        def round_tensor(pe, r, cells, lookups):
            for k in range(NC):
                kind, par, c = CELLS[k]
                at, n = cell_cols(CELLS[k])
                if cells:
                    if kind == "seq":
                        back, slot = previous_seq(k)
                        prev = before(r) if back else r
                        at_least(pe, h_low, cell_number(prev, slot))
                        at_least(pe, h_high, cell_number(prev, slot))
                        at_least(pe, seq_x_done, seqs(before(r), SEQ_SLOTS.index(k)))
                    else:
                        at_least(pe, h_low, cell_number(before(r), k))
                        at_least(pe, h_high, cell_number(before(r), k))
                        at_least(pe, nwf_x_done, sets(before(r), cell_sets(c)[-1]))
                    for g in range(4):
                        at_least(pe, gate_done, r.count(4 * NC, 4 * (k - 1 - NC) + g + 1))
                        if kind == "seq":
                            for z in range(2):
                                last = nc.tensor.matmul(g_ps[g][64 * z:64 * z + 64, :], seq_w[:, z, g, :],
                                                        seq_hx[par][z][:, at:at + n], start=True, stop=True)
                        else:
                            for m in cell_sets(c):
                                a, w = SETS[m][0] * LANES, SETS[m][1] * LANES
                                for z in range(2):
                                    last = nc.tensor.matmul(g_ps[g][64 * z:64 * z + 64, a - at:a - at + w],
                                                            nwf_w[:, z, m, g, :],
                                                            nwf_hx[1 - r.parity][z][:, a:a + w],
                                                            start=True, stop=True)
                        last.then_inc(gate_ready, 1)
                if k in SEQ_SLOTS and lookups:
                    q = SEQ_SLOTS.index(k)
                    slot = (NS * r.plus + q) % RING
                    at_least(pe, seq_onehot_ready, seqs(r, q))
                    at_least(pe, seq_x_done, seqs(r, q, -1))
                    for part in range(3):
                        for z, row in ((0, 64), (1, 0)):
                            last = nc.tensor.matmul(sx_ps[row:row + 32, :], seq_tab[:, part, :],
                                                    seq_onehot[:, slot, :].rearrange(
                                                        "p (h z c) -> p h z c", h=2, z=2)[:, :, z, :],
                                                    start=(part == 0), stop=(part == 2))
                    last.then_inc(seq_x_ready, 1)
                for prev, u in ([(r, 2 * k - 2), (r, 2 * k - 1)] if k and lookups else
                                [(before(r), NU - 2), (before(r), NU - 1)] if not k and cells else []):
                    bring(pe, prev, u)
                if lookups:
                    for u in (2 * k, 2 * k + 1):
                        ty, m, _ = UNITS[u]
                        slot = unit_of(r, u)
                        at_least(pe, onehot_ready, units(r, u))
                        at_least(pe, kept_ready, units(r, u, -2))
                        for part in range(3):
                            for g in range(4):
                                last = nc.tensor.matmul(e_ps[u % 2][32 * g:32 * g + 32, :], tab[:, part, 2 * m + ty, :],
                                                        onehot[:, slot, g * CH:(g + 1) * CH],
                                                        start=(part == 0), stop=(part == 2))
                        last.then_inc(looked_up, 1)

        def bring(pe, r, u):
            ty, m, quads = UNITS[u]
            n = SETS[m][1] * LANES
            at_least(pe, kept_ready, units(r, u))
            if ty == 0 and quads[0] == 0:
                at_least(pe, nwf_x_done, sets(r, m, -1))
            for i, q in enumerate(quads):
                last = nc.tensor.matmul(x_ps[QUAD_AT[q]:QUAD_AT[q] + 32, 0:n],
                                        cst[:, C_RED + 32 * ty:C_RED + 32 * ty + 32],
                                        kept[:, unit_of(r, u), i * n:(i + 1) * n], start=(ty == 0), stop=(ty == 1))
            last.then_inc(kept_used, 1)

        PAIRS = (NWF_T - 2) // 2

        with nc.Block() as block:

            @block.sync
            def _(sp):
                round_sync(sp, Round(None, 0, 0), 0, 0)
                round_sync(sp, Round(None, 0, 1), 1, 2)
                with sp.Fori(0, PAIRS) as i:
                    for h in range(2):
                        round_sync(sp, Round(i, 2, 2 + h), i * 2 + (2 + h), i * 4 + (4 + 2 * h))

            @block.vector
            def _(dve):
                round_vector(dve, Round(None, 0, 0), False, True, False)
                round_vector(dve, Round(None, 0, 1), True, True, True)
                with dve.Fori(0, PAIRS) as i:
                    for h in range(2):
                        round_vector(dve, Round(i, 2, 2 + h), True, True, False)
                last = Round(None, 0, NWF_T)
                round_vector(dve, last, True, False, False)
                new_h_high(dve, last, NC - 1, parity2(last, NC - 1))

            @block.gpsimd
            def _(pool):
                round_gpsimd(pool, Round(None, 0, 1), True)
                with pool.Fori(0, PAIRS) as i:
                    for h in range(2):
                        round_gpsimd(pool, Round(i, 2, 2 + h), False)
                last = Round(None, 0, NWF_T)
                round_gpsimd(pool, last, False)
                new_h_low(pool, last, NC - 1, parity2(last, NC - 1))

            @block.scalar
            def _(act):
                round_scalar(act, Round(None, 0, 0), False, True, False)
                round_scalar(act, Round(None, 0, 1), True, True, True)
                with act.Fori(0, PAIRS) as i:
                    for h in range(2):
                        round_scalar(act, Round(i, 2, 2 + h), True, True, False)
                last = Round(None, 0, NWF_T)
                round_scalar(act, last, True, False, False)
                tanh_of(act, last, NC - 1, parity2(last, NC - 1))

            @block.tensor
            def _(pe):
                round_tensor(pe, Round(None, 0, 0), False, True)
                round_tensor(pe, Round(None, 0, 1), True, True)
                with pe.Fori(0, PAIRS) as i:
                    for h in range(2):
                        round_tensor(pe, Round(i, 2, 2 + h), True, True)
                round_tensor(pe, Round(None, 0, NWF_T), True, False)

        work.close()

        end = ExitStack()
        nwf_out_w = sb("nwf_out_w", [P, 2, FEATURES, 8, OUT], F32, end)
        seq_out_w = sb("seq_out_w", [P, 2, OUT], F32, end)
        y = sb("y", [P, SLOTS, OUT], F32, end)
        y_ps = [end.enter_context(nc.psum_tensor(f"y_ps{z}", [P, 8, OUT], F32)) for z in range(2)]
        s_out_zero = sem("s_out_zero")
        s_out_w = sem("s_out_w")
        s_sum = sem("s_sum")
        s_y = sem("s_y")
        s_store = sem("s_store")
        nwf_rows = reduce_W[146:234, :].rearrange("(j u) o -> u j o", u=NWF_H)
        with nc.Block() as block:
            @block.vector
            def _(dve):
                nc.vector.memset(seq_out_w[:, :, :], 0.0)
                nc.vector.memset(nwf_out_w[:, :, :, :, :], 0.0).then_inc(s_out_zero, 1)
                for z in range(2):
                    dve.wait_ge(s_sum, z + 1)
                    nc.vector.tensor_scalar(y[:, 8 * z:8 * z + 8, :], y_ps[z][:, :, :], 0.0, None,
                                            ALU.max).then_inc(s_y, 1)

            @block.sync
            def _(sp):
                sp.wait_ge(s_out_zero, 1)
                for z in range(2):
                    sp.dma_start(seq_out_w[64 * z:64 * z + 64, z, :],
                                 reduce_W[8 + 64 * z:72 + 64 * z, :]).then_inc(s_out_w, 16)
                for s in range(SLOTS):
                    sp.dma_start(nwf_out_w[8 * s:8 * s + 8, s // 8, :, s % 8, :], nwf_rows).then_inc(s_out_w, 16)
                sp.wait_ge(s_y, 2)
                sp.dma_start(out.rearrange("(b s) o -> b s o", s=SLOTS), y[:, :, :]).then_inc(s_store, 16)
                sp.wait_ge(s_store, 16)

            @block.tensor
            def _(pe):
                pe.wait_ge(s_out_w, 16 * (SLOTS + 2))
                for z in range(2):
                    for j in range(FEATURES):
                        nc.tensor.matmul(y_ps[z][:, :, :].rearrange("b s o -> b (s o)"),
                                         nwf_hx[0][z][:, j * LANES:(j + 1) * LANES],
                                         nwf_out_w[:, z, j, :, :].rearrange("p s o -> p (s o)"),
                                         start=(j == 0), stop=False, skip_group_check=True)
                    for s in range(8 * z, 8 * z + 8):
                        for half in range(2):
                            nc.tensor.matmul(y_ps[z][:, s % 8, :],
                                             seq_hx[0][half][:, s * LANES:(s + 1) * LANES], seq_out_w[:, half, :],
                                             start=False, stop=False, skip_group_check=True)
                        last = nc.tensor.matmul(y_ps[z][:, s % 8, :],
                                                small[:, (s // 4) * LANES:(s // 4 + 1) * LANES],
                                                small_w[:, s % 4, :],
                                                start=False, stop=(s % 8 == 7), skip_group_check=True)
                    last.then_inc(s_sum, 1)
        end.close()


def constants():
    c = np.zeros((P, C_ALL), np.float32)
    c[:, C_ID:C_ID + P] = np.eye(P, dtype=np.float32)
    p = np.arange(P)
    quarter, high, dim = p // 32, (p % 32) // 4, p % 4
    for ty in range(2):
        c[p, C_RED + 32 * ty + 8 * quarter + 4 * ty + dim] = 1.0
    c[:, C_LOW] = p
    c[:, C_HIGH] = 128.0 * high
    return c


_INS = ["r_goby_idx", "r_is_indel", "r_matches_ref", "r_from_seq", "r_to_seq", "r_count_fwd", "r_count_rev",
        "r_nwf_numbers", "r_nwf_freqs", "L0_rec_goby_emb", "L0_rec_bool_emb", "L0_rec_count_emb",
        "L0_rec_base_emb", "L0_rec_seq_Wx", "L0_rec_seq_Wh", "L0_rec_seq_b", "L0_rec_nwf_num_emb",
        "L0_rec_nwf_freq_emb", "L0_rec_nwf_Wx", "L0_rec_nwf_Wh", "L0_rec_nwf_b", "L0_rec_reduce_W",
        "L0_rec_reduce_b"]


def kernel(**inputs):
    import concourse.bacc as bacc
    from concourse.bass_utils import run_bass_kernel_spmd

    nc = bacc.Bacc("TRN2", target_bir_lowering=False, num_devices=1)
    arrays, args = {}, []
    for name in _INS:
        a = np.ascontiguousarray(inputs[name])
        arrays[f"in_{name}"] = a
        args.append(nc.dram_tensor(f"in_{name}", a.shape, mybir.dt.from_np(a.dtype), kind="ExternalInput").ap())
    c = constants()
    arrays["in_consts"] = c
    args.append(nc.dram_tensor("in_consts", c.shape, F32, kind="ExternalInput").ap())
    args.append(nc.dram_tensor("out_y", (B, OUT), F32, kind="ExternalOutput").ap())
    build(nc, *args)
    r = run_bass_kernel_spmd(nc, [arrays], core_ids=[0])
    return r.results[0]["out_y"]
```

```python
from contextlib import ExitStack

import numpy as np
import concourse.bass as bass
from concourse import mybir

F32 = mybir.dt.float32
BF16 = mybir.dt.bfloat16
I32 = mybir.dt.int32
I16 = mybir.dt.int16
ALU = mybir.AluOpType
ACT = mybir.ActivationFunctionType

P = 128
B = 2048
SLOTS = B // P
LANES = P
SEQ_T, NWF_T = 64, 32
SEQ_H, SEQ_E, VOCAB = 64, 6, 85
NWF_H, NWF_E, NWF_ROWS = 8, 8, 1000
FEATURES = 11
SETS = [(0, 2), (2, 2), (4, 2), (6, 2), (8, 1), (9, 2)]
NSETS = len(SETS)
OUT = 64
GATES = [(0, ACT.Sigmoid), (2, ACT.Tanh), (1, ACT.Sigmoid), (3, ACT.Sigmoid)]
CH = 512

CELLS = [("seq", 0, 0), ("seq", 0, 1), ("seq", 0, 2), ("nwf", None, 0), ("seq", 0, 3), ("seq", 1, 0),
         ("seq", 1, 1), ("nwf", None, 1), ("seq", 1, 2), ("seq", 1, 3), ("nwf", None, 2)]
NC = len(CELLS)
NWF_CELLS = [(0, 512), (512, 512), (1024, 384)]

UNITS = []
for _m, (_f, _n) in enumerate(SETS):
    for _ty in range(2):
        for _q in ([(0, 1), (2, 3)] if _n == 2 else [(0, 1, 2, 3)]):
            UNITS.append((_ty, _m, _q))
NU = len(UNITS)
SEQ_UNITS = [(0, 0), (0, 1), (1, 0), (1, 1)]
NS = len(SEQ_UNITS)
SEQ_UNIT_SLOTS = [CELLS.index(("seq", p, 2 * c + 1)) for p, c in SEQ_UNITS]
STORED_AS = [FEATURES * ty + 2 * m - (m == 5) + (q[0] // 2) for ty, m, q in UNITS]
SET_END = [max(u for u, x in enumerate(UNITS) if x[1] == m) for m in range(NSETS)]
SET_SLOT = [e // 2 + 1 for e in SET_END]
QUAD_AT = [64, 96, 0, 32]
RING = 4

C_ID, C_RED, C_DIAG, C_LOW, C_HIGH, C_SEQ, C_FIRST, C_ALL = 0, 128, 192, 256, 257, 258, 260, 264


class Round:

    def __init__(self, i, times, plus):
        self.i, self.times, self.plus = i, times, plus

    def count(self, each, more, per=1):
        if self.i is None:
            return (each * self.plus + more) // per
        return self.i * (self.times * each // per) + (each * self.plus + more) // per

    @property
    def parity(self):
        return self.plus % 2


def at_least(eng, sem, value):
    if isinstance(value, int) and value <= 0:
        return
    eng.wait_ge(sem, value)


def unit_of(r, u):
    return (NU * r.plus + u) % RING


def build(nc, goby_idx, is_indel, matches_ref, from_seq, to_seq, count_fwd, count_rev, numbers, freqs,
          goby_emb, bool_emb, count_emb, base_emb, seq_Wx, seq_Wh, seq_b, num_emb, freq_emb,
          nwf_Wx, nwf_Wh, nwf_b, reduce_W, reduce_b, consts, out):
    ctx = ExitStack()
    with ctx:
        def sb(name, shape, dt, stack=ctx):
            return stack.enter_context(nc.sbuf_tensor(name, shape, dt))

        def sem(name):
            return ctx.enter_context(nc.semaphore(name))

        low_dram = nc.dram_tensor("low_digits", [NWF_T, NU, 4, CH], BF16, kind="Internal").ap()
        high_dram = nc.dram_tensor("high_digits", [NWF_T, NU, 4, CH], BF16, kind="Internal").ap()
        tok_dram = nc.dram_tensor("seq_tokens", [SEQ_T, SLOTS // 2, 2, 2, LANES], BF16, kind="Internal").ap()

        cst = sb("cst", [P, C_ALL], F32)
        seq_hx = [[sb(f"seq_hx{p}{z}", [P, B], F32) for z in range(2)] for p in range(2)]
        seq_c = sb("seq_c", [P, B], F32)
        nwf_hx = [[sb(f"nwf_hx{p}{z}", [P, FEATURES * LANES], F32) for z in range(2)] for p in range(2)]
        nwf_c = sb("nwf_c", [P, FEATURES * LANES], F32)
        seq_w = sb("seq_w", [P, 2, 4, SEQ_H], F32)
        nwf_out_w = sb("nwf_out_w", [P, FEATURES, 8, OUT], F32)
        seq_out_w = sb("seq_out_w", [P, 2, OUT], F32)
        nwf_w = sb("nwf_w", [P, 2, NSETS, 4, 64], F32)
        nwf_bias = sb("nwf_bias", [P, NSETS, 4], F32)
        tab = sb("tab", [P, 3, 2 * NSETS, 32], BF16)
        seq_tab = sb("seq_tab", [P, 2, 32], BF16)
        small_rows = sb("small_rows", [P, SLOTS, 32], F32)
        few_idx = sb("few_idx", [P, 5, SLOTS], I32)
        small_w = sb("small_w", [P, 4, OUT], F32)

        prep = ExitStack()
        nidx = FEATURES * SLOTS * NWF_T
        nwf_in = [nwf_out_w[:, :, :, :].rearrange("p j s o -> p (j s o)").bitcast(I32),
                  sb("nwf_in1", [P, nidx], I32, prep)[:, :]]
        seq_in = [seq_c[:, k * SLOTS * SEQ_T:(k + 1) * SLOTS * SEQ_T].bitcast(I32) for k in range(2)]
        near = sb("near", [P, nidx], I16, prep)
        wrap = sb("wrap", [P, nidx], I16, prep)
        dig = [sb(f"dig{k}", [P, nidx], BF16, prep) for k in range(2)]
        turned = [sb(f"turned{k}", [P, nidx], BF16, prep) for k in range(2)]
        ident_bf = sb("ident_bf", [P, P], BF16, prep)
        tab_f = sb("tab_f", [P, 2 * NSETS + 2, 32], F32, prep)
        tab_r = sb("tab_r", [P, 2 * NSETS + 2, 32], F32, prep)
        tab_p = sb("tab_p", [P, 3, 2 * NSETS + 2, 32], BF16, prep)
        base_p = sb("base_p", [P, 2, 32], F32, prep)
        nwf_rows = sb("nwf_rows", [P, NSETS * 4, 8], F32, prep)
        few_in = sb("few_in", [P, 5, SLOTS], I32, prep)
        few_f = sb("few_f", [P, 5, SLOTS], F32, prep)
        tp = [prep.enter_context(nc.psum_tensor(f"tp{n}", [P, 4, LANES], BF16)) for n in range(4)]

        s_cst = sem("s_cst")
        s_few = sem("s_few")
        s_in = [sem(f"s_in{k}") for k in range(4)]
        s_zero = sem("s_zero")
        s_base = sem("s_base")
        s_weights = sem("s_weights")
        s_tables = sem("s_tables")
        s_out_w = sem("s_out_w")
        s_gather = sem("s_gather")
        s_few_idx = sem("s_few_idx")
        s_small_set = sem("s_small_set")
        s_digits = sem("s_digits")
        s_turned = sem("s_turned")
        s_evicted = sem("s_evicted")
        s_stored = [sem(f"s_stored{k}") for k in range(2)]
        s_chain = sem("s_chain")

        PASSES = [(0, "seq"), (1, "seq"), (2, "low"), (2, "high"), (3, "low"), (3, "high")]
        GROUPS = [2] * 2 + [FEATURES] * 4
        STORES = [2] * 2 + [4] * 4
        groups_before = [sum(GROUPS[:n]) for n in range(len(PASSES) + 1)]

        def stores_before(n):
            return sum(STORES[m] for m in range(n) if m % 2 == n % 2)

        def turned_at(n, grp):
            flat = turned[n % 2][:, :]
            if n < 2:
                return flat[:, grp * CH:(grp + 1) * CH].rearrange("p (q l) -> p q l", q=4)
            if grp == 8:
                return flat[:, 8 * CH:9 * CH].rearrange("p (q l) -> p q l", q=4)
            at, i = ((grp // 2) * 2 * CH, grp % 2) if grp < 8 else (9 * CH, grp - 9)
            return flat[:, at:at + 2 * CH].rearrange("p (q i l) -> p q i l", q=4, i=2)[:, :, i, :]

        weight_dmas, table_dmas, out_dmas = [], [], []
        for z in range(2):
            hrow, xrow = (0, 64) if z == 0 else (64, 0)
            for row, rows, w in ((hrow, SEQ_H, seq_Wh), (xrow, SEQ_E, seq_Wx), (xrow + SEQ_E, 1, seq_b[None, :])):
                weight_dmas.append((seq_w[row:row + rows, z, :, :].rearrange("p g u -> p (g u)"), w))
        for s in range(8):
            for base, w in ((0, nwf_Wh), (64, nwf_Wx)):
                weight_dmas.append((nwf_rows[base + 8 * s:base + 8 * s + 8, :, :].rearrange(
                    "p (m g) u -> p m (g u)", m=NSETS), w.rearrange("m d c -> d m c")))
        for ty, src in enumerate((num_emb, freq_emb)):
            for m in range(NSETS):
                t = tab_f[:, 2 * m + ty, :].rearrange("p (a d) -> p a d", d=4)
                table_dmas.append((t[:, 0:7, :], src[m, 0:7 * P, :].rearrange("(a b) d -> b a d", b=P)))
                table_dmas.append((t[0:NWF_ROWS - 7 * P, 7, :], src[m, 7 * P:NWF_ROWS, :]))
        cut = P - VOCAB
        for dst, src in ((tab_f[0:VOCAB, 2 * NSETS, 0:SEQ_E], base_emb),
                         (tab_f[VOCAB:P, 2 * NSETS, 0:SEQ_E], base_emb[0:cut, :]),
                         (tab_f[0:VOCAB - cut, 2 * NSETS + 1, 0:SEQ_E], base_emb[cut:VOCAB, :]),
                         (tab_f[VOCAB - cut:2 * VOCAB - cut, 2 * NSETS + 1, 0:SEQ_E], base_emb)):
            table_dmas.append((dst, src))
        for r in range(4):
            out_dmas.append((small_w[32 * r:32 * r + 8, r, :], reduce_W[0:8, :]))
            out_dmas.append((small_w[32 * r + 8:32 * r + 18, r, :], reduce_W[136:146, :]))
            out_dmas.append((small_w[32 * r + 18:32 * r + 19, r, :], reduce_b[None, :]))
        for z in range(2):
            out_dmas.append((seq_out_w[64 * z:64 * z + 64, z, :], reduce_W[8 + 64 * z:72 + 64 * z, :]))
        for s in range(SLOTS):
            out_dmas.append((nwf_out_w[8 * s:8 * s + 8, :, s % 8, :],
                             reduce_W[146:234, :].rearrange("(j u) o -> u j o", u=NWF_H)))

        def gather_small(pool, places):
            for n, s in places:
                table = (goby_emb, bool_emb, bool_emb, count_emb, count_emb)[n]
                at, width = ((0, 4), (4, 2), (6, 2), (8, 5), (13, 5))[n]
                nc.gpsimd.indirect_dma_start(
                    out=small_rows[:, s, at:at + width], out_offset=None, in_=table,
                    in_offset=bass.IndirectOffsetOnAxis(ap=few_idx[:, n, s:s + 1], axis=0)).then_inc(s_gather, 16)

        SMALL = [(n, s) for n in range(5) for s in range(SLOTS)]
        EARLY = 60

        with nc.Block() as block:
            @block.sync
            def _(sp):
                for n, src in enumerate((goby_idx, is_indel, matches_ref, count_fwd, count_rev)):
                    sp.dma_start(few_in[:, n, :], src.rearrange("(b s) -> b s", s=SLOTS)).then_inc(s_few, 16)
                for k, src in enumerate((from_seq, to_seq)):
                    sp.dma_start(seq_in[k], src.rearrange("(b s) t -> b (s t)", s=SLOTS)).then_inc(s_in[k], 16)
                sp.dma_start(cst[:, :], consts).then_inc(s_cst, 16)
                for k, src in enumerate((numbers, freqs)):
                    sp.dma_start(nwf_in[k].rearrange("p (j c) -> p j c", j=FEATURES),
                                 src.rearrange("j (b s) t -> b j (s t)", s=SLOTS)).then_inc(s_in[2 + k], 16)
                sp.wait_ge(s_zero, 1)
                for dst, src in table_dmas:
                    sp.dma_start(dst, src).then_inc(s_tables, 16)
                for dst, src in weight_dmas:
                    sp.dma_start(dst, src).then_inc(s_weights, 16)
                for s in range(SLOTS):
                    sp.dma_start(nwf_bias[8 * s:8 * s + 8, :, :], nwf_b.rearrange("m (g u) -> u m g", g=4),
                                 allow_slow_non_contiguous=True).then_inc(s_weights, 16)
                sp.wait_ge(s_weights, 16 * (len(weight_dmas) + SLOTS))

            @block.scalar
            def _(act):
                for n, (k, kind) in enumerate(PASSES):
                    half = turned[n % 2]
                    if n >= 2:
                        act.wait_ge(s_stored[n % 2], 16 * stores_before(n))
                    for grp in range(GROUPS[n]):
                        at = groups_before[n] + grp
                        act.wait_ge(s_turned, at + 1)
                        nc.scalar.copy(turned_at(n, grp), tp[at % 4][:, :, :]).then_inc(s_evicted, 1)
                    act.wait_ge(s_evicted, groups_before[n + 1])
                    if kind != "seq":
                        dram = low_dram if kind == "low" else high_dram
                        for r in range(4):
                            act.dma_start(dram[:, FEATURES * (k - 2):FEATURES * (k - 1), r, :],
                                          half[32 * r:32 * r + 32, :].rearrange("p (u c) -> p u c", c=CH)
                                          ).then_inc(s_stored[n % 2], 16)
                    else:
                        for odd in range(2):
                            act.dma_start(tok_dram[:, :, k, odd, :],
                                          half[64 * odd:64 * odd + 64, 0:8 * LANES]
                                          .rearrange("p (h l) -> p h l", h=8)).then_inc(s_stored[n % 2], 16)
                for k in range(2):
                    act.wait_ge(s_stored[k], 16 * stores_before(len(PASSES) + k))

            @block.gpsimd
            def _(pool):
                nc.gpsimd.memset(small_rows[:, :, :], 0.0).then_inc(s_small_set, 1)
                pool.wait_ge(s_small_set, 1)
                nc.gpsimd.memset(small_rows[:, :, 18:19], 1.0).then_inc(s_small_set, 1)
                for p in range(2):
                    for z in range(2):
                        nc.gpsimd.memset(seq_hx[p][z][:, :], 0.0)
                nc.gpsimd.memset(nwf_c[:, :], 0.0)
                pool.wait_ge(s_small_set, 2)
                pool.wait_ge(s_few_idx, 1)
                gather_small(pool, SMALL[:EARLY])

            @block.vector
            def _(dve):
                chain = [0]

                def link(ins):
                    chain[0] += 1
                    ins.then_inc(s_chain, 1)
                    dve.wait_ge(s_chain, chain[0])

                nc.vector.memset(tab_f[:, :, :], 0.0)
                nc.vector.memset(seq_w[:, :, :, :], 0.0).then_inc(s_zero, 1)

                def in_range(near, wrap, src, rows):
                    link(nc.vector.tensor_scalar(near, src, float(-rows), float(rows - 1), ALU.max, ALU.min))
                    link(nc.vector.tensor_scalar(wrap, near, 0.0, float(rows), ALU.is_lt, ALU.mult))
                    link(nc.vector.tensor_tensor(near, near, wrap, ALU.add))

                dve.wait_ge(s_few, 16 * 5)
                for n, rows in enumerate((100, 2, 2, 12500, 12500)):
                    in_range(few_f[:, n, :], few_idx[:, n, :], few_in[:, n, :], rows)
                nc.vector.tensor_copy(few_idx[:, :, :], few_f[:, :, :]).then_inc(s_few_idx, 1)
                for z in range(2):
                    nc.vector.memset(nwf_hx[0][z][:, :], 0.0)
                dve.wait_ge(s_cst, 16)
                link(nc.vector.tensor_copy(ident_bf[:, :], cst[:, C_ID:C_ID + P]))

                for n, (k, kind) in enumerate(PASSES):
                    w = SLOTS * SEQ_T if k < 2 else nidx
                    if kind != "high":
                        dve.wait_ge(s_in[k], 16)
                        in_range(near[:, 0:w], wrap[:, 0:w], seq_in[k] if k < 2 else nwf_in[k - 2],
                                 VOCAB if k < 2 else NWF_ROWS)
                    if n >= 2:
                        dve.wait_ge(s_turned, groups_before[n - 1])
                    digit = near
                    if kind != "seq":
                        link(nc.vector.tensor_scalar(wrap[:, 0:w], near[:, 0:w], 127 if kind == "low" else 896, None,
                                                     ALU.bitwise_and))
                        digit = wrap
                    nc.vector.tensor_copy(dig[n % 2][:, 0:w], digit[:, 0:w]).then_inc(s_digits, 1)
                    dve.wait_ge(s_digits, n + 1)
                nc.vector.memset(seq_c[:, :], 0.0)
                dve.wait_ge(s_tables, 16 * len(table_dmas))
                link(nc.vector.memset(tab_f[:, 2 * NSETS:, SEQ_E:SEQ_E + 1], 1.0))
                left, rest = tab_f, tab_r
                for part in range(3):
                    link(nc.vector.tensor_copy(tab_p[:, part, :, :], left[:, :, :]))
                    if part < 2:
                        link(nc.vector.tensor_tensor(rest[:, :, :], left[:, :, :], tab_p[:, part, :, :], ALU.subtract))
                    left, rest = rest, left
                nc.vector.tensor_copy(tab[:, :, :, :], tab_p[:, :, 0:2 * NSETS, :])
                for n in range(2):
                    one, other = tab_p[:, n, 2 * NSETS + n, :], tab_p[:, n + 1, 2 * NSETS + n, :]
                    link(nc.vector.tensor_scalar(base_p[:, n, :], one, cst[:, C_FIRST + 2 * n:C_FIRST + 2 * n + 1],
                                                 None, ALU.mult))
                    nc.vector.scalar_tensor_tensor(out=seq_tab[:, n, :], in0=other,
                                                   scalar=cst[:, C_FIRST + 2 * n + 1:C_FIRST + 2 * n + 2],
                                                   in1=base_p[:, n, :], op0=ALU.mult, op1=ALU.add)
                dve.wait_ge(s_weights, 16 * (len(weight_dmas) + SLOTS))
                for z in range(2):
                    for part in range(2):
                        src = slice(64 * part, 64 * part + 64)
                        row = 64 * (part ^ z)
                        link(nc.vector.tensor_tensor(
                            nwf_w[row:row + 64, z, :, :, :].rearrange("p m g (s u) -> p (m g) s u", u=8),
                            nwf_rows[src, :, None, :].to_broadcast([64, NSETS * 4, 8, 8]),
                            cst[src, None, C_DIAG:C_DIAG + 64].rearrange("p o (s u) -> p o s u", u=8)
                            .to_broadcast([64, NSETS * 4, 8, 8]), ALU.mult))

            @block.tensor
            def _(pe):
                for n in range(len(PASSES)):
                    pe.wait_ge(s_digits, n + 1)
                    for grp in range(GROUPS[n]):
                        at = groups_before[n] + grp
                        if at >= 4:
                            pe.wait_ge(s_evicted, at - 3)
                        for q in range(4):
                            block_at = (4 * grp + q) * P
                            last = nc.tensor.transpose(tp[at % 4][:, q, :], dig[n % 2][:, block_at:block_at + P],
                                                       ident_bf[:, :])
                        last.then_inc(s_turned, 1)

        prep.close()

        work = ExitStack()
        low = sb("low", [P, RING, 4 * CH], BF16, work)
        high = sb("high", [P, RING, CH], BF16, work)
        onehot = sb("onehot", [P, RING, 4 * CH], BF16, work)
        kept = sb("kept", [P, RING, CH], F32, work)
        tok = sb("tok", [P, 2, 4 * CH], BF16, work)
        seq_onehot = sb("seq_onehot", [P, 2, 4 * CH], BF16, work)
        gates = [[sb(f"gate{g}{p}", [P, CH], F32, work) for p in range(2)] for g in range(4)]
        ig = sb("ig", [P, 2, CH], F32, work)
        tanh_c = sb("tanh_c", [P, 2, CH], F32, work)

        g_ps = [work.enter_context(nc.psum_tensor(f"g_ps{g}", [P, CH], F32)) for g in range(4)]
        e_ps = [work.enter_context(nc.psum_tensor(f"e_ps{n}", [P, CH], F32)) for n in range(2)]
        x_ps = work.enter_context(nc.psum_tensor("x_ps", [P, CH], F32))
        sx_ps = work.enter_context(nc.psum_tensor("sx_ps", [P, CH], F32))

        low_here = [sem(f"low_here{n}") for n in range(2)]
        high_here = [sem(f"high_here{n}") for n in range(2)]
        tokens_here = [sem(f"tokens_here{n}") for n in range(2)]
        onehot_ready = sem("onehot_ready")
        seq_onehot_ready = sem("seq_onehot_ready")
        looked_up = sem("looked_up")
        kept_ready = sem("kept_ready")
        kept_used = sem("kept_used")
        nwf_x_done = sem("nwf_x_done")
        seq_onehot_used = sem("seq_onehot_used")
        seq_x_done = sem("seq_x_done")
        out_zero = sem("out_zero")
        x_cleared = sem("x_cleared")
        gate_ready = sem("gate_ready")
        gate_done = sem("gate_done")
        ig_ready = sem("ig_ready")
        c_scaled = sem("c_scaled")
        c_ready = sem("c_ready")
        tanh_ready = sem("tanh_ready")
        h_low = sem("h_low")
        h_high = sem("h_high")

        def cell_number(r, k, more=0):
            return r.count(NC, k + more + 1 - NC)

        def units(r, u, more=0):
            return r.count(NU, u + 1 + more)

        def sets(r, m, more=0):
            return r.count(NSETS, m + 1 + more)

        def seqs(r, q, more=0):
            return r.count(NS, q + 1 + more)

        def before(r):
            return Round(r.i, r.times, r.plus - 1)

        def cell_cols(cell):
            kind, _, c = cell
            return (c * CH, CH) if kind == "seq" else NWF_CELLS[c]

        def cell_sets(c):
            return [m for m, (f, n) in enumerate(SETS) if NWF_CELLS[c][0] <= f * LANES < sum(NWF_CELLS[c])]

        def previous_seq(k):
            _, p, c = CELLS[k]
            return (1 - p, next(n for n, x in enumerate(CELLS) if x == ("seq", 1 - p, c)))


        def round_sync(sp, r, step, seq_step):
            for k in range(NC):
                if k in SEQ_UNIT_SLOTS:
                    q = SEQ_UNIT_SLOTS.index(k)
                    par, c = SEQ_UNITS[q]
                    at_least(sp, seq_onehot_ready, 2 * seqs(r, q, -2))
                    sp.dma_start(tok[:, q % 2, :],
                                 tok_dram[bass.ds(seq_step + par, 1), 4 * c:4 * c + 4, :, :, :]
                                 .rearrange("t h z o l -> t (h z o l)")
                                 .to_broadcast([P, 4 * CH])).then_inc(tokens_here[q % 2], 16)
                at, pair = unit_of(r, 2 * k), pair_slot(r, k)
                one, other = STORED_AS[2 * k], STORED_AS[2 * k + 1]
                both = slice(one, other + 1, other - one)
                at_least(sp, onehot_ready, units(r, 2 * k + 1, -RING))
                sp.dma_start(low[:, at:at + 2, :],
                             low_dram[bass.ds(step, 1), both, :, :].rearrange("t u r c -> t u (r c)")
                             .to_broadcast([P, 2, 4 * CH])).then_inc(low_here[pair], 16)
                at_least(sp, kept_ready, units(r, 2 * k + 1, -RING))
                for g in range(4):
                    sp.dma_start(high[32 * g:32 * g + 32, at:at + 2, :],
                                 high_dram[bass.ds(step, 1), both, g, :]
                                 .to_broadcast([32, 2, CH])).then_inc(high_here[pair], 16)

        def pair_slot(r, k):
            return unit_of(r, 2 * k) // 2

        def pair_fills(r, k, each):
            return (each * ((NU * r.plus + 2 * k) // RING + 1)
                    + (0 if r.i is None else r.i * (each * r.times * NU // RING)))

        def keep_wanted(dve, r, u):
            at = unit_of(r, u)
            at_least(dve, high_here[at // 2], pair_fills(r, u // 2, 4 * 16))
            at_least(dve, looked_up, units(r, u))
            at_least(dve, kept_used, units(r, u, -RING))
            nc.vector.scalar_tensor_tensor(out=kept[:, at, :], in0=high[:, at, :], scalar=cst[:, C_HIGH:C_HIGH + 1],
                                           in1=e_ps[u % 2][:, :], op0=ALU.is_equal,
                                           op1=ALU.mult).then_inc(kept_ready, 1)

        def new_h(k, r):
            kind, par, c = CELLS[k]
            at, n = cell_cols(CELLS[k])
            if kind == "seq":
                return seq_hx[1 - par][0][0:64, at:at + n], seq_hx[1 - par][1][64:128, at:at + n]
            return nwf_hx[r.parity][0][0:64, at:at + n], nwf_hx[r.parity][1][64:128, at:at + n]

        def new_h_low(pool, r, k, slot2):
            _, n = cell_cols(CELLS[k])
            at_least(pool, tanh_ready, cell_number(r, k))
            nc.gpsimd.tensor_tensor(new_h(k, r)[0], gates[3][slot2][0:64, 0:n], tanh_c[0:64, slot2, 0:n],
                                    ALU.mult).then_inc(h_low, 1)

        def new_h_high(dve, r, k, slot2):
            _, n = cell_cols(CELLS[k])
            at_least(dve, tanh_ready, cell_number(r, k))
            nc.vector.tensor_tensor(new_h(k, r)[1], gates[3][slot2][64:128, 0:n], tanh_c[64:128, slot2, 0:n],
                                    ALU.mult).then_inc(h_high, 1)

        def c_of(k):
            at, n = cell_cols(CELLS[k])
            return (seq_c if CELLS[k][0] == "seq" else nwf_c)[:, at:at + n], n

        def parity2(r, k):
            return (NC * (r.plus - 1) + k) % 2

        def cell_before(r, k):
            return (r, k - 1) if k else (before(r), NC - 1)

        def round_vector(dve, r, cells, lookups, first):
            for k in range(NC):
                if k in SEQ_UNIT_SLOTS and lookups:
                    q = SEQ_UNIT_SLOTS.index(k)
                    at_least(dve, tokens_here[q % 2], r.count(16 * NS, 16 * (q - q % 2 + 2), 2))
                    for n in range(2):
                        at_least(dve, seq_onehot_used, 2 * seqs(r, q, -1) + n - 1)
                        nc.vector.tensor_scalar(seq_onehot[:, n, :], tok[:, q % 2, :],
                                                cst[:, C_SEQ + n:C_SEQ + n + 1], None,
                                                ALU.is_equal).then_inc(seq_onehot_ready, 1)
                if k > 0 and lookups:
                    keep_wanted(dve, r, 2 * k - 2)
                    keep_wanted(dve, r, 2 * k - 1)
                if k == 0 and cells:
                    keep_wanted(dve, before(r), NU - 2)
                    keep_wanted(dve, before(r), NU - 1)
                if lookups:
                    for u in (2 * k, 2 * k + 1):
                        at = unit_of(r, u)
                        at_least(dve, low_here[at // 2], pair_fills(r, k, 16))
                        at_least(dve, looked_up, units(r, u, -RING))
                        nc.vector.tensor_scalar(onehot[:, at, :], low[:, at, :], cst[:, C_LOW:C_LOW + 1], None,
                                                ALU.is_equal).then_inc(onehot_ready, 1)
                if cells:
                    two = parity2(r, k)
                    c, n = c_of(k)
                    at_least(dve, gate_done, r.count(4 * NC, 4 * (k - NC) + 3))
                    nc.vector.tensor_tensor(c, c, gates[2][two][:, 0:n], ALU.mult).then_inc(c_scaled, 1)
                    if not (first and k == 0):
                        new_h_high(dve, *cell_before(r, k), 1 - two)
                    at_least(dve, c_scaled, cell_number(r, k))
                    at_least(dve, ig_ready, cell_number(r, k))
                    nc.vector.tensor_tensor(c, c, ig[:, two, 0:n], ALU.add).then_inc(c_ready, 1)

        def round_gpsimd(pool, r, first):
            for k in range(NC):
                two = parity2(r, k)
                _, n = cell_cols(CELLS[k])
                at_least(pool, gate_done, r.count(4 * NC, 4 * (k - NC) + 2))
                at_least(pool, c_ready, cell_number(r, k, -2))
                nc.gpsimd.tensor_tensor(ig[:, two, 0:n], gates[0][two][:, 0:n], gates[1][two][:, 0:n],
                                        ALU.mult).then_inc(ig_ready, 1)
                if not (first and k == 0):
                    new_h_low(pool, *cell_before(r, k), 1 - two)

        def tanh_of(act, r, k, slot2):
            c, n = c_of(k)
            at_least(act, c_ready, cell_number(r, k))
            nc.scalar.activation(tanh_c[:, slot2, 0:n], c, ACT.Tanh).then_inc(tanh_ready, 1)

        def store_x(act, r, m):
            f, count = SETS[m]
            at, n = f * LANES, count * LANES
            at_least(act, kept_used, units(r, SET_END[m]))
            hx = nwf_hx[r.parity]
            nc.scalar.copy(hx[0][64:128, at:at + n], x_ps[64:128, 0:n])
            nc.scalar.copy(hx[1][0:64, at:at + n], x_ps[0:64, 0:n]).then_inc(nwf_x_done, 1)

        def round_scalar(act, r, cells, lookups, first):
            for k in range(NC):
                kind, par, c = CELLS[k]
                if cells:
                    two = parity2(r, k)
                    at_least(act, h_low, cell_number(r, k, -2))
                    at_least(act, h_high, cell_number(r, k, -2))
                    at, n = cell_cols(CELLS[k])
                    for g, (place, func) in enumerate(GATES):
                        at_least(act, gate_ready, r.count(4 * NC, 4 * (k - NC) + g + 1))
                        if kind == "seq":
                            last = nc.scalar.activation(gates[g][two][:, :], g_ps[g][:, :], func)
                        else:
                            for m in cell_sets(c):
                                a, w = SETS[m][0] * LANES - at, SETS[m][1] * LANES
                                last = nc.scalar.activation(gates[g][two][:, a:a + w], g_ps[g][:, a:a + w], func,
                                                            bias=nwf_bias[:, m, place:place + 1])
                        last.then_inc(gate_done, 1)
                    if not (first and k == 0):
                        tanh_of(act, *cell_before(r, k), 1 - two)
                if k in SEQ_UNIT_SLOTS and lookups:
                    q = SEQ_UNIT_SLOTS.index(k)
                    upar, pair = SEQ_UNITS[q]
                    at_least(act, seq_onehot_used, 2 * seqs(r, q))
                    for z, row in ((0, 64), (1, 0)):
                        for i in range(2):
                            at = (2 * pair + i) * CH
                            last = nc.scalar.copy(seq_hx[upar][z][row:row + 32, at:at + CH],
                                                  sx_ps[row + 32 * i:row + 32 * i + 32, :])
                    last.then_inc(seq_x_done, 1)
                for m in range(NSETS):
                    if lookups and SET_SLOT[m] == k:
                        store_x(act, r, m)
                    if cells and SET_SLOT[m] - NC == k:
                        store_x(act, before(r), m)

        def round_tensor(pe, r, cells, lookups):
            for k in range(NC):
                kind, par, c = CELLS[k]
                at, n = cell_cols(CELLS[k])
                if cells:
                    if kind == "seq":
                        back, slot = previous_seq(k)
                        prev = before(r) if back else r
                        at_least(pe, h_low, cell_number(prev, slot))
                        at_least(pe, h_high, cell_number(prev, slot))
                        at_least(pe, seq_x_done, seqs(before(r), SEQ_UNITS.index((par, c // 2))))
                    else:
                        at_least(pe, h_low, cell_number(before(r), k))
                        at_least(pe, h_high, cell_number(before(r), k))
                        at_least(pe, nwf_x_done, sets(before(r), cell_sets(c)[-1]))
                    for g, (place, _) in enumerate(GATES):
                        at_least(pe, gate_done, r.count(4 * NC, 4 * (k - 1 - NC) + g + 1))
                        if kind == "seq":
                            for z in range(2):
                                last = nc.tensor.matmul(g_ps[g][64 * z:64 * z + 64, :], seq_w[:, z, place, :],
                                                        seq_hx[par][z][:, at:at + n], start=True, stop=True)
                        else:
                            for m in cell_sets(c):
                                a, w = SETS[m][0] * LANES, SETS[m][1] * LANES
                                for z in range(2):
                                    last = nc.tensor.matmul(g_ps[g][64 * z:64 * z + 64, a - at:a - at + w],
                                                            nwf_w[:, z, m, place, :],
                                                            nwf_hx[1 - r.parity][z][:, a:a + w],
                                                            start=True, stop=True)
                        last.then_inc(gate_ready, 1)
                if k in SEQ_UNIT_SLOTS and lookups:
                    q = SEQ_UNIT_SLOTS.index(k)
                    at_least(pe, seq_x_done, seqs(r, q, -1))
                    for part in range(2):
                        at_least(pe, seq_onehot_ready, 2 * seqs(r, q, -1) + part + 1)
                        view = seq_onehot[:, part, :].rearrange("p (c h z l) -> p c h z l", c=2, h=2, z=2)
                        for z, row in ((0, 64), (1, 0)):
                            for i in range(2):
                                last = nc.tensor.matmul(sx_ps[row + 32 * i:row + 32 * i + 32, :], seq_tab[:, part, :],
                                                        view[:, i, :, z, :], start=(part == 0), stop=(part == 1))
                        last.then_inc(seq_onehot_used, 1)
                for prev, u in ([(r, 2 * k - 2), (r, 2 * k - 1)] if k and lookups else
                                [(before(r), NU - 2), (before(r), NU - 1)] if not k and cells else []):
                    bring(pe, prev, u)
                if lookups:
                    for u in (2 * k, 2 * k + 1):
                        ty, m, _ = UNITS[u]
                        slot = unit_of(r, u)
                        at_least(pe, onehot_ready, units(r, u))
                        at_least(pe, kept_ready, units(r, u, -2))
                        for part in range(3):
                            for g in range(4):
                                last = nc.tensor.matmul(e_ps[u % 2][32 * g:32 * g + 32, :], tab[:, part, 2 * m + ty, :],
                                                        onehot[:, slot, g * CH:(g + 1) * CH],
                                                        start=(part == 0), stop=(part == 2))
                        last.then_inc(looked_up, 1)

        def bring(pe, r, u):
            ty, m, quads = UNITS[u]
            n = SETS[m][1] * LANES
            at_least(pe, kept_ready, units(r, u))
            if ty == 0 and quads[0] == 0:
                at_least(pe, nwf_x_done, sets(r, m, -1))
            for i, q in enumerate(quads):
                last = nc.tensor.matmul(x_ps[QUAD_AT[q]:QUAD_AT[q] + 32, 0:n],
                                        cst[:, C_RED + 32 * ty:C_RED + 32 * ty + 32],
                                        kept[:, unit_of(r, u), i * n:(i + 1) * n], start=(ty == 0), stop=(ty == 1))
            last.then_inc(kept_used, 1)

        PAIRS = (NWF_T - 2) // 2

        with nc.Block() as block:

            @block.sync
            def _(sp):
                round_sync(sp, Round(None, 0, 0), 0, 0)
                sp.wait_ge(out_zero, 1)
                for dst, src in out_dmas:
                    sp.dma_start(dst, src).then_inc(s_out_w, 16)
                round_sync(sp, Round(None, 0, 1), 1, 2)
                with sp.Fori(0, PAIRS) as i:
                    for h in range(2):
                        round_sync(sp, Round(i, 2, 2 + h), i * 2 + (2 + h), i * 4 + (4 + 2 * h))
                sp.wait_ge(s_out_w, 16 * len(out_dmas))

            @block.vector
            def _(dve):
                round_vector(dve, Round(None, 0, 0), False, True, False)
                round_vector(dve, Round(None, 0, 1), True, True, True)
                with dve.Fori(0, PAIRS) as i:
                    for h in range(2):
                        round_vector(dve, Round(i, 2, 2 + h), True, True, False)
                last = Round(None, 0, NWF_T)
                round_vector(dve, last, True, False, False)
                new_h_high(dve, last, NC - 1, parity2(last, NC - 1))

            @block.gpsimd
            def _(pool):
                nc.gpsimd.memset(small_w[:, :, :], 0.0)
                nc.gpsimd.memset(seq_out_w[:, :, :], 0.0)
                nc.gpsimd.memset(nwf_out_w[:, :, :, :], 0.0).then_inc(out_zero, 1)
                gather_small(pool, SMALL[EARLY:])
                round_gpsimd(pool, Round(None, 0, 1), True)
                with pool.Fori(0, PAIRS) as i:
                    for h in range(2):
                        round_gpsimd(pool, Round(i, 2, 2 + h), False)
                last = Round(None, 0, NWF_T)
                pool.wait_ge(h_high, cell_number(before(last), NC - 1))
                nc.gpsimd.memset(nwf_hx[0][1][0:64, :], 0.0)
                nc.gpsimd.memset(nwf_hx[0][0][64:128, :], 0.0).then_inc(x_cleared, 1)
                pool.wait_ge(x_cleared, 1)
                round_gpsimd(pool, last, False)
                new_h_low(pool, last, NC - 1, parity2(last, NC - 1))

            @block.scalar
            def _(act):
                round_scalar(act, Round(None, 0, 0), False, True, False)
                round_scalar(act, Round(None, 0, 1), True, True, True)
                with act.Fori(0, PAIRS) as i:
                    for h in range(2):
                        round_scalar(act, Round(i, 2, 2 + h), True, True, False)
                last = Round(None, 0, NWF_T)
                round_scalar(act, last, True, False, False)
                tanh_of(act, last, NC - 1, parity2(last, NC - 1))

            @block.tensor
            def _(pe):
                round_tensor(pe, Round(None, 0, 0), False, True)
                round_tensor(pe, Round(None, 0, 1), True, True)
                with pe.Fori(0, PAIRS) as i:
                    for h in range(2):
                        round_tensor(pe, Round(i, 2, 2 + h), True, True)
                round_tensor(pe, Round(None, 0, NWF_T), True, False)

        work.close()

        end = ExitStack()
        small = sb("small", [P, 4 * LANES], F32, end)
        y = sb("y", [P, SLOTS, OUT], F32, end)
        y_ps = [end.enter_context(nc.psum_tensor(f"y_ps{z}", [P, 8, OUT], F32)) for z in range(2)]
        small_ps = end.enter_context(nc.psum_tensor("small_ps", [P, 4 * LANES], F32))
        s_small_t = sem("s_small_t")
        s_small = sem("s_small")
        s_sum = sem("s_sum")
        s_y = sem("s_y")
        s_store = sem("s_store")
        with nc.Block() as block:
            @block.scalar
            def _(act):
                act.wait_ge(s_small_t, 1)
                nc.scalar.copy(small[:, :], small_ps[:, :]).then_inc(s_small, 1)

            @block.vector
            def _(dve):
                for z in range(2):
                    dve.wait_ge(s_sum, z + 1)
                    nc.vector.tensor_scalar(y[:, 8 * z:8 * z + 8, :], y_ps[z][:, :, :], 0.0, None,
                                            ALU.max).then_inc(s_y, 1)

            @block.sync
            def _(sp):
                for z in range(2):
                    sp.wait_ge(s_y, z + 1)
                    sp.dma_start(out.rearrange("(b s) o -> b s o", s=SLOTS)[:, 8 * z:8 * z + 8, :],
                                 y[:, 8 * z:8 * z + 8, :]).then_inc(s_store, 16)
                sp.wait_ge(s_store, 32)

            @block.tensor
            def _(pe):
                pe.wait_ge(s_gather, 16 * len(SMALL))
                rows = small_rows[:, :, :].rearrange("b s d -> b (s d)")
                for q in range(4):
                    last = nc.tensor.transpose(small_ps[:, q * LANES:(q + 1) * LANES], rows[:, q * P:(q + 1) * P],
                                               cst[:, C_ID:C_ID + P])
                last.then_inc(s_small_t, 1)
                for z in range(2):
                    for j in range(FEATURES):
                        nc.tensor.matmul(y_ps[z][:, :, :].rearrange("b s o -> b (s o)"),
                                         nwf_hx[0][z][:, j * LANES:(j + 1) * LANES],
                                         nwf_out_w[:, j, :, :].rearrange("p s o -> p (s o)"),
                                         start=(j == 0), stop=False, skip_group_check=True)
                    if z == 0:
                        pe.wait_ge(s_small, 1)
                    for s in range(8 * z, 8 * z + 8):
                        for half in range(2):
                            nc.tensor.matmul(y_ps[z][:, s % 8, :],
                                             seq_hx[0][half][:, s * LANES:(s + 1) * LANES], seq_out_w[:, half, :],
                                             start=False, stop=False, skip_group_check=True)
                        last = nc.tensor.matmul(y_ps[z][:, s % 8, :],
                                                small[:, (s // 4) * LANES:(s // 4 + 1) * LANES],
                                                small_w[:, s % 4, :],
                                                start=False, stop=(s % 8 == 7), skip_group_check=True)
                    last.then_inc(s_sum, 1)
        end.close()


def constants():
    c = np.zeros((P, C_ALL), np.float32)
    c[:, C_ID:C_ID + P] = np.eye(P, dtype=np.float32)
    p = np.arange(P)
    quarter, high, dim = p // 32, (p % 32) // 4, p % 4
    for ty in range(2):
        c[p, C_RED + 32 * ty + 8 * quarter + 4 * ty + dim] = 1.0
    c[:, C_DIAG:C_DIAG + 64] = (p[:, None] % 64) // 8 == np.arange(64)[None, :] // 8
    c[:, C_LOW] = p
    part = (VOCAB, P - VOCAB, 2 * VOCAB - P)
    c[:, C_SEQ] = np.where(p < part[0], p, p - part[0])
    c[:, C_SEQ + 1] = np.where(p < part[2], p + part[1], np.where(p < part[2] + VOCAB, p - part[2], -1))
    for n, rows in enumerate((part[0], part[2])):
        c[:, C_FIRST + 2 * n] = p < rows
        c[:, C_FIRST + 2 * n + 1] = p >= rows
    c[:, C_HIGH] = 128.0 * high
    return c


_INS = ["r_goby_idx", "r_is_indel", "r_matches_ref", "r_from_seq", "r_to_seq", "r_count_fwd", "r_count_rev",
        "r_nwf_numbers", "r_nwf_freqs", "L0_rec_goby_emb", "L0_rec_bool_emb", "L0_rec_count_emb",
        "L0_rec_base_emb", "L0_rec_seq_Wx", "L0_rec_seq_Wh", "L0_rec_seq_b", "L0_rec_nwf_num_emb",
        "L0_rec_nwf_freq_emb", "L0_rec_nwf_Wx", "L0_rec_nwf_Wh", "L0_rec_nwf_b", "L0_rec_reduce_W",
        "L0_rec_reduce_b"]


def kernel(**inputs):
    import concourse.bacc as bacc
    from concourse.bass_utils import run_bass_kernel_spmd

    nc = bacc.Bacc("TRN2", target_bir_lowering=False, num_devices=1)
    arrays, args = {}, []
    for name in _INS:
        a = np.ascontiguousarray(inputs[name])
        arrays[f"in_{name}"] = a
        args.append(nc.dram_tensor(f"in_{name}", a.shape, mybir.dt.from_np(a.dtype), kind="ExternalInput").ap())
    c = constants()
    arrays["in_consts"] = c
    args.append(nc.dram_tensor("in_consts", c.shape, F32, kind="ExternalInput").ap())
    args.append(nc.dram_tensor("out_y", (B, OUT), F32, kind="ExternalOutput").ap())
    build(nc, *args)
    r = run_bass_kernel_spmd(nc, [arrays], core_ids=[0])
    return r.results[0]["out_y"]
```

```python
from contextlib import ExitStack

import numpy as np
import concourse.bass as bass
from concourse import mybir

F32 = mybir.dt.float32
BF16 = mybir.dt.bfloat16
I32 = mybir.dt.int32
I16 = mybir.dt.int16
ALU = mybir.AluOpType
ACT = mybir.ActivationFunctionType

P = 128
B = 2048
SLOTS = B // P
LANES = P
SEQ_T, NWF_T = 64, 32
SEQ_H, SEQ_E, VOCAB = 64, 6, 85
NWF_H, NWF_E, NWF_ROWS = 8, 8, 1000
FEATURES = 11
SETS = [(0, 2), (2, 2), (4, 2), (6, 2), (8, 1), (9, 2)]
NSETS = len(SETS)
OUT = 64
GATES = [(0, ACT.Sigmoid), (2, ACT.Tanh), (1, ACT.Sigmoid), (3, ACT.Sigmoid)]
CH = 512

CELLS = [("seq", 0, 0), ("seq", 0, 1), ("seq", 0, 2), ("nwf", None, 0), ("seq", 0, 3), ("seq", 1, 0),
         ("seq", 1, 1), ("nwf", None, 1), ("seq", 1, 2), ("seq", 1, 3), ("nwf", None, 2)]
NC = len(CELLS)
SEQ_SLOTS = [k for k, x in enumerate(CELLS) if x[0] == "seq"]
NWF_SLOTS = [k for k, x in enumerate(CELLS) if x[0] == "nwf"]
NWF_CELLS = [(0, 512), (512, 512), (1024, 384)]

UNITS = []
for _m, (_f, _n) in enumerate(SETS):
    for _ty in range(2):
        for _q in ([(0, 1), (2, 3)] if _n == 2 else [(0, 1, 2, 3)]):
            UNITS.append((_ty, _m, _q))
NU = len(UNITS)
SEQ_UNITS = [(0, 0), (0, 1), (1, 0), (1, 1)]
NS = len(SEQ_UNITS)
SEQ_UNIT_SLOTS = [CELLS.index(("seq", p, 2 * c + 1)) for p, c in SEQ_UNITS]
STORED_AS = [FEATURES * ty + 2 * m - (m == 5) + (q[0] // 2) for ty, m, q in UNITS]
SET_END = [max(u for u, x in enumerate(UNITS) if x[1] == m) for m in range(NSETS)]
SET_SLOT = [e // 2 + 1 for e in SET_END]
QUAD_AT = [64, 96, 0, 32]
RING = 4
LOW_BASE, LOW_BITS = 128.0, 0x4300
HIGH_BASE, HIGH_BITS = 2.0, 0x4000
SMALL_DIMS = 19
REST = FEATURES * NWF_H + SMALL_DIMS

C_ID, C_RED, C_DIAG, C_LOW, C_HIGH, C_SEQ, C_FIRST, C_ALL = 0, 128, 192, 256, 257, 258, 260, 264


class Round:

    def __init__(self, i, times, plus):
        self.i, self.times, self.plus = i, times, plus

    def count(self, each, more, per=1):
        if self.i is None:
            return (each * self.plus + more) // per
        return self.i * (self.times * each // per) + (each * self.plus + more) // per

    @property
    def parity(self):
        return self.plus % 2

    @property
    def slots(self):
        if self.i is None and self.plus == 0:
            return SEQ_SLOTS
        if self.i is None and self.plus == NWF_T:
            return NWF_SLOTS
        return list(range(NC))

    @property
    def lookups(self):
        return self.i is not None or self.plus < NWF_T

    @property
    def seq_lookups(self):
        return self.i is not None or self.plus < SEQ_T // 2 - 1


def at_least(eng, sem, value):
    if isinstance(value, int) and value <= 0:
        return
    eng.wait_ge(sem, value)


def unit_of(r, u):
    return (NU * r.plus + u) % RING


def build(nc, goby_idx, is_indel, matches_ref, from_seq, to_seq, count_fwd, count_rev, numbers, freqs,
          goby_emb, bool_emb, count_emb, base_emb, seq_Wx, seq_Wh, seq_b, num_emb, freq_emb,
          nwf_Wx, nwf_Wh, nwf_b, reduce_W, reduce_b, consts, out):
    ctx = ExitStack()
    with ctx:
        def sb(name, shape, dt, stack=ctx):
            return stack.enter_context(nc.sbuf_tensor(name, shape, dt))

        def sem(name):
            return ctx.enter_context(nc.semaphore(name))

        low_dram = nc.dram_tensor("low_digits", [NWF_T, NU, 4, CH], BF16, kind="Internal").ap()
        high_dram = nc.dram_tensor("high_digits", [NWF_T, NU, 4, CH], BF16, kind="Internal").ap()
        tok_dram = nc.dram_tensor("seq_tokens", [SEQ_T, SLOTS // 2, 2, 2, LANES], BF16, kind="Internal").ap()
        h_dram = nc.dram_tensor("last_h", [SLOTS, NWF_H, FEATURES * LANES], F32, kind="Internal").ap()

        cst = sb("cst", [P, C_ALL], F32)
        seq_hx = [[sb(f"seq_hx{p}{z}", [P, B], F32) for z in range(2)] for p in range(2)]
        seq_c = sb("seq_c", [P, B], F32)
        nwf_hx_all = sb("nwf_hx", [P, 2, 2, FEATURES * LANES], F32)
        nwf_hx = [[nwf_hx_all[:, p, z, :] for z in range(2)] for p in range(2)]
        nwf_c = sb("nwf_c", [P, FEATURES * LANES], F32)
        seq_w = sb("seq_w", [P, 2, 4, SEQ_H], F32)
        seq_out_w = sb("seq_out_w", [P, 2, OUT], F32)
        nwf_w = sb("nwf_w", [P, 2, NSETS, 4, 64], F32)
        nwf_bias = sb("nwf_bias", [P, NSETS, 4], F32)
        tab = sb("tab", [P, 3, 2 * NSETS, 32], BF16)
        seq_tab = sb("seq_tab", [P, 2, 32], BF16)
        rest_w = sb("rest_w", [REST, OUT], F32)
        small_rows = sb("small_rows", [P, SLOTS, 32], F32)
        few_idx = sb("few_idx", [P, 5, SLOTS], I32)
        nwf_rows = sb("nwf_rows", [P, NSETS * 4, 8], F32)
        tok = sb("tok", [P, 2, 4 * CH], BF16)
        seq_onehot = sb("seq_onehot", [P, 2, 4 * CH], BF16)
        index_space = sb("index_space", [P, FEATURES * SLOTS * NWF_T], I32)
        y_at, rest_at = 4 * LANES, 4 * LANES + SLOTS * OUT
        small = index_space[:, 0:y_at].bitcast(F32)
        y = index_space[:, y_at:rest_at].bitcast(F32).rearrange("b (s o) -> b s o", s=SLOTS)
        rest = index_space[0:REST, rest_at:rest_at + B].bitcast(F32).rearrange("k (s b) -> k s b", s=SLOTS)
        sx_ps = ctx.enter_context(nc.psum_tensor("sx_ps", [P, CH], F32))

        tokens_here = [sem(f"tokens_here{n}") for n in range(2)]
        seq_onehot_ready = sem("seq_onehot_ready")
        seq_onehot_used = sem("seq_onehot_used")
        seq_x_done = sem("seq_x_done")

        def seqs(r, q, more=0):
            return r.count(NS, q + 1 + more + NS)

        def load_tokens(sp, r, q, seq_step):
            par, c = SEQ_UNITS[q]
            at_least(sp, seq_onehot_ready, 2 * seqs(r, q, -2))
            sp.dma_start(tok[:, q % 2, :],
                         tok_dram[bass.ds(seq_step + par, 1), 4 * c:4 * c + 4, :, :, :]
                         .rearrange("t h z o l -> t (h z o l)")
                         .to_broadcast([P, 4 * CH])).then_inc(tokens_here[q % 2], 16)

        def seq_compare(dve, r, q):
            at_least(dve, tokens_here[q % 2], r.count(16 * NS, 16 * (q - q % 2 + 2 + NS), 2))
            for n in range(2):
                at_least(dve, seq_onehot_used, 2 * seqs(r, q, -1) + n - 1)
                nc.vector.tensor_scalar(seq_onehot[:, n, :], tok[:, q % 2, :],
                                        cst[:, C_SEQ + n:C_SEQ + n + 1], None,
                                        ALU.is_equal).then_inc(seq_onehot_ready, 1)

        def seq_products(pe, r, q):
            at_least(pe, seq_x_done, seqs(r, q, -1))
            for part in range(2):
                at_least(pe, seq_onehot_ready, 2 * seqs(r, q, -1) + part + 1)
                view = seq_onehot[:, part, :].rearrange("p (c h z l) -> p c h z l", c=2, h=2, z=2)
                for z, row in ((0, 64), (1, 0)):
                    for i in range(2):
                        last = nc.tensor.matmul(sx_ps[row + 32 * i:row + 32 * i + 32, :], seq_tab[:, part, :],
                                                view[:, i, :, z, :], start=(part == 0), stop=(part == 1))
                last.then_inc(seq_onehot_used, 1)

        def store_seq_x(act, r, q):
            par, pair = SEQ_UNITS[q]
            at_least(act, seq_onehot_used, 2 * seqs(r, q))
            for z, row in ((0, 64), (1, 0)):
                for i in range(2):
                    at = (2 * pair + i) * CH
                    last = nc.scalar.copy(seq_hx[par][z][row:row + 32, at:at + CH],
                                          sx_ps[row + 32 * i:row + 32 * i + 32, :])
            last.then_inc(seq_x_done, 1)

        prep = ExitStack()
        nidx = FEATURES * SLOTS * NWF_T
        nwf_in = [index_space[:, :],
                  nwf_hx_all[:, :, :, :].rearrange("p a z c -> p (a z c)").bitcast(I32)]
        seq_in = [seq_c[:, k * SLOTS * SEQ_T:(k + 1) * SLOTS * SEQ_T].bitcast(I32) for k in range(2)]
        near = sb("near", [P, nidx], I16, prep)
        wrap = sb("wrap", [P, nidx], I16, prep)
        dig = [sb(f"dig{k}", [P, nidx], BF16, prep) for k in range(2)]
        turned = [sb(f"turned{k}", [P, nidx], BF16, prep) for k in range(2)]
        ident_bf = sb("ident_bf", [P, P], BF16, prep)
        tab_f = sb("tab_f", [P, 2 * NSETS + 2, 32], F32, prep)
        tab_r = sb("tab_r", [P, 2 * NSETS + 2, 32], F32, prep)
        tab_p = sb("tab_p", [P, 3, 2 * NSETS + 2, 32], BF16, prep)
        base_p = sb("base_p", [P, 2, 32], F32, prep)
        few_in = sb("few_in", [P, 5, SLOTS], I32, prep)
        few_f = sb("few_f", [P, 5, SLOTS], F32, prep)
        tp = [prep.enter_context(nc.psum_tensor(f"tp{n}", [P, 4, LANES], BF16)) for n in range(4)]

        s_cst = sem("s_cst")
        s_few = sem("s_few")
        s_in = [sem(f"s_in{k}") for k in range(4)]
        s_zero = sem("s_zero")
        s_state = sem("s_state")
        s_seq_tab = sem("s_seq_tab")
        s_weights = sem("s_weights")
        s_tables = sem("s_tables")
        s_late = sem("s_late")
        s_gather = sem("s_gather")
        s_few_idx = sem("s_few_idx")
        s_small_set = sem("s_small_set")
        s_digits = sem("s_digits")
        s_turned = sem("s_turned")
        s_evicted = sem("s_evicted")
        s_stored = [sem(f"s_stored{k}") for k in range(2)]
        s_chain = sem("s_chain")

        PASSES = [(0, "seq"), (1, "seq"), (2, "low"), (2, "high"), (3, "low"), (3, "high")]
        GROUPS = [2] * 2 + [FEATURES] * 4
        STORES = [2] * 2 + [4] * 4
        groups_before = [sum(GROUPS[:n]) for n in range(len(PASSES) + 1)]

        def stores_before(n):
            return sum(STORES[m] for m in range(n) if m % 2 == n % 2)

        def turned_at(n, grp):
            flat = turned[n % 2][:, :]
            if n < 2:
                return flat[:, grp * CH:(grp + 1) * CH].rearrange("p (q l) -> p q l", q=4)
            if grp == 8:
                return flat[:, 8 * CH:9 * CH].rearrange("p (q l) -> p q l", q=4)
            at, i = ((grp // 2) * 2 * CH, grp % 2) if grp < 8 else (9 * CH, grp - 9)
            return flat[:, at:at + 2 * CH].rearrange("p (q i l) -> p q i l", q=4, i=2)[:, :, i, :]

        def store_pass(sp, n):
            k, kind = PASSES[n]
            half = turned[n % 2]
            sp.wait_ge(s_evicted, groups_before[n + 1])
            if kind == "seq":
                for odd in range(2):
                    sp.dma_start(tok_dram[:, :, k, odd, :], half[64 * odd:64 * odd + 64, 0:8 * LANES]
                                 .rearrange("p (h l) -> p h l", h=8)).then_inc(s_stored[n % 2], 16)
            else:
                dram = low_dram if kind == "low" else high_dram
                for r in range(4):
                    sp.dma_start(dram[:, FEATURES * (k - 2):FEATURES * (k - 1), r, :],
                                 half[32 * r:32 * r + 32, :].rearrange("p (u c) -> p u c", c=CH)
                                 ).then_inc(s_stored[n % 2], 16)

        seq_weight_dmas, nwf_weight_dmas, table_dmas, out_dmas, late_dmas = [], [], [], [], []
        for z in range(2):
            hrow, xrow = (0, 64) if z == 0 else (64, 0)
            for row, rows, w in ((hrow, SEQ_H, seq_Wh), (xrow, SEQ_E, seq_Wx), (xrow + SEQ_E, 1, seq_b[None, :])):
                seq_weight_dmas.append((seq_w[row:row + rows, z, :, :].rearrange("p g u -> p (g u)"), w))
        for s in range(8):
            for base, w in ((0, nwf_Wh), (64, nwf_Wx)):
                nwf_weight_dmas.append((nwf_rows[base + 8 * s:base + 8 * s + 8, :, :].rearrange(
                    "p (m g) u -> p m (g u)", m=NSETS), w.rearrange("m d c -> d m c")))
        for ty, src in enumerate((num_emb, freq_emb)):
            for m in range(NSETS):
                t = tab_f[:, 2 * m + ty, :].rearrange("p (a d) -> p a d", d=4)
                table_dmas.append((t[:, 0:7, :], src[m, 0:7 * P, :].rearrange("(a b) d -> b a d", b=P)))
                table_dmas.append((t[0:NWF_ROWS - 7 * P, 7, :], src[m, 7 * P:NWF_ROWS, :]))
        cut = P - VOCAB
        for dst, src in ((tab_f[0:VOCAB, 2 * NSETS, 0:SEQ_E], base_emb),
                         (tab_f[VOCAB:P, 2 * NSETS, 0:SEQ_E], base_emb[0:cut, :]),
                         (tab_f[0:VOCAB - cut, 2 * NSETS + 1, 0:SEQ_E], base_emb[cut:VOCAB, :]),
                         (tab_f[VOCAB - cut:2 * VOCAB - cut, 2 * NSETS + 1, 0:SEQ_E], base_emb)):
            table_dmas.append((dst, src))
        for at, src in ((0, reduce_W[146:234, :]), (88, reduce_W[0:8, :]), (96, reduce_W[136:146, :]),
                        (106, reduce_b[None, :])):
            out_dmas.append((rest_w[at:at + src.shape[0], :], src))
        for z in range(2):
            out_dmas.append((seq_out_w[64 * z:64 * z + 64, z, :], reduce_W[8 + 64 * z:72 + 64 * z, :]))

        for s in range(SLOTS):
            late_dmas.append((nwf_bias[8 * s:8 * s + 8, :, :], nwf_b.rearrange("m (g u) -> u m g", g=4)))
        late_dmas += out_dmas

        def gather_small(pool, places):
            for n, s in places:
                table = (goby_emb, bool_emb, bool_emb, count_emb, count_emb)[n]
                at, width = ((0, 4), (4, 2), (6, 2), (8, 5), (13, 5))[n]
                nc.gpsimd.indirect_dma_start(
                    out=small_rows[:, s, at:at + width], out_offset=None, in_=table,
                    in_offset=bass.IndirectOffsetOnAxis(ap=few_idx[:, n, s:s + 1], axis=0)).then_inc(s_gather, 16)

        SMALL = [(n, s) for n in range(5) for s in range(SLOTS)]
        EARLY = 36
        LATE = 2
        EARLY_SEQ = 2

        with nc.Block() as block:
            @block.sync
            def _(sp):
                for n, src in enumerate((goby_idx, is_indel, matches_ref, count_fwd, count_rev)):
                    sp.dma_start(few_in[:, n, :], src.rearrange("(b s) -> b s", s=SLOTS)).then_inc(s_few, 16)
                for k, src in enumerate((from_seq, to_seq)):
                    sp.dma_start(seq_in[k], src.rearrange("(b s) t -> b (s t)", s=SLOTS)).then_inc(s_in[k], 16)
                sp.dma_start(cst[:, :], consts).then_inc(s_cst, 16)
                for k, src in enumerate((numbers, freqs)):
                    sp.dma_start(nwf_in[k].rearrange("p (j c) -> p j c", j=FEATURES),
                                 src.rearrange("j (b s) t -> b j (s t)", s=SLOTS)).then_inc(s_in[2 + k], 16)
                for n in range(2):
                    store_pass(sp, n)
                sp.wait_ge(s_zero, 1)
                for dst, src in table_dmas:
                    sp.dma_start(dst, src).then_inc(s_tables, 16)
                for dst, src in seq_weight_dmas:
                    sp.dma_start(dst, src).then_inc(s_weights, 16)
                store_pass(sp, 2)
                for n in range(2):
                    sp.wait_ge(s_stored[n], 16 * STORES[n])
                for q in range(EARLY_SEQ):
                    load_tokens(sp, Round(None, 0, -1), q, 0)
                store_pass(sp, 3)
                for dst, src in nwf_weight_dmas:
                    sp.dma_start(dst, src).then_inc(s_weights, 16)
                store_pass(sp, 4)
                store_pass(sp, 5)
                for q in range(EARLY_SEQ, NS):
                    load_tokens(sp, Round(None, 0, -1), q, 0)
                sp.wait_ge(s_weights, 16 * (len(seq_weight_dmas) + len(nwf_weight_dmas)))
                for n in range(2):
                    sp.wait_ge(s_stored[n], 16 * stores_before(len(PASSES) + n))

            @block.scalar
            def _(act):
                for n, (k, kind) in enumerate(PASSES):
                    if n >= 2:
                        act.wait_ge(s_stored[n % 2], 16 * stores_before(n))
                    for grp in range(GROUPS[n]):
                        at = groups_before[n] + grp
                        act.wait_ge(s_turned, at + 1)
                        nc.scalar.copy(turned_at(n, grp), tp[at % 4][:, :, :]).then_inc(s_evicted, 1)
                act.wait_ge(s_state, 1)
                for q in range(EARLY_SEQ):
                    store_seq_x(act, Round(None, 0, -1), q)

            @block.gpsimd
            def _(pool):
                nc.gpsimd.memset(small_rows[:, :, :], 0.0).then_inc(s_small_set, 1)
                pool.wait_ge(s_small_set, 1)
                nc.gpsimd.memset(small_rows[:, :, 18:19], 1.0).then_inc(s_small_set, 1)
                for p in range(2):
                    for z in range(2):
                        last = nc.gpsimd.memset(seq_hx[p][z][:, :], 0.0)
                last.then_inc(s_state, 1)
                nc.gpsimd.memset(nwf_c[:, :], 0.0)
                pool.wait_ge(s_small_set, 2)
                pool.wait_ge(s_few_idx, 1)
                gather_small(pool, SMALL[:EARLY])
                pool.wait_ge(s_digits, 5)
                nc.gpsimd.memset(seq_c[:, :], 0.0)
                nc.gpsimd.memset(nwf_hx_all[:, 0, :, :], 0.0)

            @block.vector
            def _(dve):
                chain = [0]

                def link(ins):
                    chain[0] += 1
                    ins.then_inc(s_chain, 1)
                    dve.wait_ge(s_chain, chain[0])

                nc.vector.memset(tab_f[:, :, :], 0.0)
                nc.vector.memset(seq_out_w[:, :, :], 0.0)
                nc.vector.memset(seq_w[:, :, :, :], 0.0).then_inc(s_zero, 1)

                def in_range(near, wrap, src, rows):
                    link(nc.vector.tensor_scalar(near, src, float(-rows), float(rows - 1), ALU.max, ALU.min))
                    link(nc.vector.tensor_scalar(wrap, near, 0.0, float(rows), ALU.is_lt, ALU.mult))
                    link(nc.vector.tensor_tensor(near, near, wrap, ALU.add))

                dve.wait_ge(s_few, 16 * 5)
                for n, rows in enumerate((100, 2, 2, 12500, 12500)):
                    in_range(few_f[:, n, :], few_idx[:, n, :], few_in[:, n, :], rows)
                nc.vector.tensor_copy(few_idx[:, :, :], few_f[:, :, :]).then_inc(s_few_idx, 1)
                dve.wait_ge(s_cst, 16)
                link(nc.vector.tensor_copy(ident_bf[:, :], cst[:, C_ID:C_ID + P]))

                for n, (k, kind) in enumerate(PASSES):
                    w = SLOTS * SEQ_T if k < 2 else nidx
                    if kind != "high":
                        dve.wait_ge(s_in[k], 16)
                        in_range(near[:, 0:w], wrap[:, 0:w], seq_in[k] if k < 2 else nwf_in[k - 2],
                                 VOCAB if k < 2 else NWF_ROWS)
                    if n >= 2:
                        dve.wait_ge(s_turned, groups_before[n - 1])
                    if kind == "seq":
                        last = nc.vector.tensor_copy(dig[n % 2][:, 0:w], near[:, 0:w])
                    else:
                        mask, bits = (127, LOW_BITS) if kind == "low" else (7 << 7, HIGH_BITS)
                        last = nc.vector.tensor_scalar(dig[n % 2][:, 0:w].bitcast(I16), near[:, 0:w], mask, bits,
                                                       ALU.bitwise_and, ALU.bitwise_or)
                    last.then_inc(s_digits, 1)
                    dve.wait_ge(s_digits, n + 1)
                dve.wait_ge(s_tables, 16 * len(table_dmas))
                link(nc.vector.memset(tab_f[:, 2 * NSETS:, SEQ_E:SEQ_E + 1], 1.0))
                left, rest = tab_f, tab_r
                for part in range(3):
                    link(nc.vector.tensor_copy(tab_p[:, part, :, :], left[:, :, :]))
                    if part < 2:
                        link(nc.vector.tensor_tensor(rest[:, :, :], left[:, :, :], tab_p[:, part, :, :], ALU.subtract))
                    left, rest = rest, left
                nc.vector.tensor_copy(tab[:, :, :, :], tab_p[:, :, 0:2 * NSETS, :])
                for n in range(2):
                    one, other = tab_p[:, n, 2 * NSETS + n, :], tab_p[:, n + 1, 2 * NSETS + n, :]
                    link(nc.vector.tensor_scalar(base_p[:, n, :], one, cst[:, C_FIRST + 2 * n:C_FIRST + 2 * n + 1],
                                                 None, ALU.mult))
                    nc.vector.scalar_tensor_tensor(out=seq_tab[:, n, :], in0=other,
                                                   scalar=cst[:, C_FIRST + 2 * n + 1:C_FIRST + 2 * n + 2],
                                                   in1=base_p[:, n, :], op0=ALU.mult,
                                                   op1=ALU.add).then_inc(s_seq_tab, 1)
                for q in range(EARLY_SEQ):
                    seq_compare(dve, Round(None, 0, -1), q)

            @block.tensor
            def _(pe):
                for n in range(len(PASSES)):
                    pe.wait_ge(s_digits, n + 1)
                    for grp in range(GROUPS[n]):
                        at = groups_before[n] + grp
                        if at >= 4:
                            pe.wait_ge(s_evicted, at - 3)
                        for q in range(4):
                            block_at = (4 * grp + q) * P
                            last = nc.tensor.transpose(tp[at % 4][:, q, :], dig[n % 2][:, block_at:block_at + P],
                                                       ident_bf[:, :])
                        last.then_inc(s_turned, 1)
                pe.wait_ge(s_seq_tab, 2)
                for q in range(EARLY_SEQ):
                    seq_products(pe, Round(None, 0, -1), q)

        prep.close()

        work = ExitStack()
        low = sb("low", [P, RING, 4 * CH], BF16, work)
        high = sb("high", [P, RING, CH], BF16, work)
        onehot = sb("onehot", [P, RING, 4 * CH], BF16, work)
        kept = sb("kept", [P, RING, CH], F32, work)
        gates = [[sb(f"gate{g}{p}", [P, CH], F32, work) for p in range(2)] for g in range(4)]
        ig = sb("ig", [P, 2, CH], F32, work)
        tanh_c = sb("tanh_c", [P, 2, CH], F32, work)

        g_ps = [work.enter_context(nc.psum_tensor(f"g_ps{g}", [P, CH], F32)) for g in range(4)]
        e_ps = [work.enter_context(nc.psum_tensor(f"e_ps{n}", [P, CH], F32)) for n in range(2)]
        x_ps = work.enter_context(nc.psum_tensor("x_ps", [P, CH], F32))

        low_here = [sem(f"low_here{n}") for n in range(2)]
        high_here = [sem(f"high_here{n}") for n in range(2)]
        onehot_ready = sem("onehot_ready")
        looked_up = sem("looked_up")
        kept_ready = sem("kept_ready")
        kept_used = sem("kept_used")
        nwf_x_done = sem("nwf_x_done")
        gate_ready = sem("gate_ready")
        gate_done = sem("gate_done")
        ig_ready = sem("ig_ready")
        c_scaled = sem("c_scaled")
        c_ready = sem("c_ready")
        tanh_ready = sem("tanh_ready")
        h_low = sem("h_low")
        h_high = sem("h_high")

        h_in_dram = [sem(f"h_in_dram{c}") for c in range(3)]
        rest_here = sem("rest_here")
        nwf_w_ready = sem("nwf_w_ready")
        small_turned = sem("small_turned")
        small_ready = sem("small_ready")
        y_summed = sem("y_summed")
        y_ready = sem("y_ready")
        y_stored = sem("y_stored")

        def cell_number(r, k, more=0, each=1, plus=0):
            if r.i is not None:
                return r.count(each * NC, each * (k + 1 - len(NWF_SLOTS) + more) + plus)
            if k not in r.slots:
                return 0
            earlier = NC * r.plus - len(NWF_SLOTS) if r.plus else 0
            return each * (earlier + r.slots.index(k) + 1 + more) + plus

        def gate_number(r, k, g):
            return cell_number(r, k, -1, 4, g + 1)

        def units(r, u, more=0):
            return r.count(NU, u + 1 + more)

        def sets(r, m, more=0):
            return r.count(NSETS, m + 1 + more)

        def before(r):
            return Round(r.i, r.times, r.plus - 1)

        def has_before(r):
            return r.i is not None or r.plus > 0

        def cell_cols(cell):
            kind, _, c = cell
            return (c * CH, CH) if kind == "seq" else NWF_CELLS[c]

        def cell_sets(c):
            return [m for m, (f, n) in enumerate(SETS) if NWF_CELLS[c][0] <= f * LANES < sum(NWF_CELLS[c])]

        def previous_seq(k):
            _, p, c = CELLS[k]
            return (1 - p, next(n for n, x in enumerate(CELLS) if x == ("seq", 1 - p, c)))

        def late_seq_unit(r, k):
            return EARLY_SEQ + k if r.i is None and r.plus == 0 and EARLY_SEQ + k < NS else None

        def round_sync(sp, r, step, seq_step):
            for k in range(NC):
                if k in SEQ_UNIT_SLOTS and r.seq_lookups:
                    load_tokens(sp, r, SEQ_UNIT_SLOTS.index(k), seq_step)
                if r.i is None and r.plus == 0:
                    for dst, src in late_dmas[k::NC]:
                        sp.dma_start(dst, src, allow_slow_non_contiguous=True).then_inc(s_late, 16)
                at, pair = unit_of(r, 2 * k), pair_slot(r, k)
                one, other = STORED_AS[2 * k], STORED_AS[2 * k + 1]
                both = slice(one, other + 1, other - one)
                at_least(sp, onehot_ready, units(r, 2 * k + 1, -RING))
                sp.dma_start(low[:, at:at + 2, :],
                             low_dram[bass.ds(step, 1), both, :, :].rearrange("t u r c -> t u (r c)")
                             .to_broadcast([P, 2, 4 * CH])).then_inc(low_here[pair], 16)
                at_least(sp, kept_ready, units(r, 2 * k + 1, -RING))
                for g in range(4):
                    sp.dma_start(high[32 * g:32 * g + 32, at:at + 2, :],
                                 high_dram[bass.ds(step, 1), both, g, :]
                                 .to_broadcast([32, 2, CH])).then_inc(high_here[pair], 16)

        def pair_slot(r, k):
            return unit_of(r, 2 * k) // 2

        def pair_fills(r, k, each):
            return (each * ((NU * r.plus + 2 * k) // RING + 1)
                    + (0 if r.i is None else r.i * (each * r.times * NU // RING)))

        def keep_wanted(dve, r, u):
            at = unit_of(r, u)
            at_least(dve, high_here[at // 2], pair_fills(r, u // 2, 4 * 16))
            at_least(dve, looked_up, units(r, u))
            at_least(dve, kept_used, units(r, u, -RING))
            nc.vector.scalar_tensor_tensor(out=kept[:, at, :], in0=high[:, at, :], scalar=cst[:, C_HIGH:C_HIGH + 1],
                                           in1=e_ps[u % 2][:, :], op0=ALU.is_equal,
                                           op1=ALU.mult).then_inc(kept_ready, 1)

        def new_h(k, r):
            kind, par, c = CELLS[k]
            at, n = cell_cols(CELLS[k])
            if kind == "seq":
                return seq_hx[1 - par][0][0:64, at:at + n], seq_hx[1 - par][1][64:128, at:at + n]
            return nwf_hx[r.parity][0][0:64, at:at + n], nwf_hx[r.parity][1][64:128, at:at + n]

        def new_h_low(pool, r, k, slot2):
            _, n = cell_cols(CELLS[k])
            at_least(pool, tanh_ready, cell_number(r, k))
            nc.gpsimd.tensor_tensor(new_h(k, r)[0], gates[3][slot2][0:64, 0:n], tanh_c[0:64, slot2, 0:n],
                                    ALU.mult).then_inc(h_low, 1)

        def new_h_high(dve, r, k, slot2):
            _, n = cell_cols(CELLS[k])
            at_least(dve, tanh_ready, cell_number(r, k))
            nc.vector.tensor_tensor(new_h(k, r)[1], gates[3][slot2][64:128, 0:n], tanh_c[64:128, slot2, 0:n],
                                    ALU.mult).then_inc(h_high, 1)

        def c_of(k):
            at, n = cell_cols(CELLS[k])
            return (seq_c if CELLS[k][0] == "seq" else nwf_c)[:, at:at + n], n

        def parity2(r, k):
            return (NC * r.plus - len(NWF_SLOTS) + k) % 2 if r.i is not None else (cell_number(r, k) - 1) % 2

        def cell_before(r, k):
            n = r.slots.index(k)
            if not n and r.i is None and r.plus == 0:
                return None
            prev, slot = (r, r.slots[n - 1]) if n else (before(r), before(r).slots[-1])
            return prev, slot, parity2(prev, slot)

        PLACE_AT = [2, 3, 4, 5]

        def place_nwf_w(dve, z, part):
            src = slice(64 * part, 64 * part + 64)
            row = 64 * (part ^ z)
            nc.vector.tensor_tensor(
                nwf_w[row:row + 64, z, :, :, :].rearrange("p m g (s u) -> p (m g) s u", u=8),
                nwf_rows[src, :, None, :].to_broadcast([64, NSETS * 4, 8, 8]),
                cst[src, None, C_DIAG:C_DIAG + 64].rearrange("p o (s u) -> p o s u", u=8)
                .to_broadcast([64, NSETS * 4, 8, 8]), ALU.mult).then_inc(nwf_w_ready, 1)

        def round_vector(dve, r):
            for k in range(NC):
                if late_seq_unit(r, k):
                    seq_compare(dve, before(r), late_seq_unit(r, k))
                if k in SEQ_UNIT_SLOTS and r.seq_lookups:
                    seq_compare(dve, r, SEQ_UNIT_SLOTS.index(k))
                if k > 0 and r.lookups:
                    keep_wanted(dve, r, 2 * k - 2)
                    keep_wanted(dve, r, 2 * k - 1)
                if k == 0 and has_before(r):
                    keep_wanted(dve, before(r), NU - 2)
                    keep_wanted(dve, before(r), NU - 1)
                if r.i is None and r.plus == 0 and k in PLACE_AT:
                    place_nwf_w(dve, *divmod(PLACE_AT.index(k), 2))
                if r.lookups:
                    for u in (2 * k, 2 * k + 1):
                        at = unit_of(r, u)
                        at_least(dve, low_here[at // 2], pair_fills(r, k, 16))
                        at_least(dve, looked_up, units(r, u, -RING))
                        nc.vector.tensor_scalar(onehot[:, at, :], low[:, at, :], cst[:, C_LOW:C_LOW + 1], None,
                                                ALU.is_equal).then_inc(onehot_ready, 1)
                if k in r.slots:
                    two = parity2(r, k)
                    c, n = c_of(k)
                    at_least(dve, gate_done, gate_number(r, k, 2))
                    nc.vector.tensor_tensor(c, c, gates[2][two][:, 0:n], ALU.mult).then_inc(c_scaled, 1)
                    if cell_before(r, k):
                        new_h_high(dve, *cell_before(r, k))
                    at_least(dve, c_scaled, cell_number(r, k))
                    at_least(dve, ig_ready, cell_number(r, k))
                    nc.vector.tensor_tensor(c, c, ig[:, two, 0:n], ALU.add).then_inc(c_ready, 1)

        def round_gpsimd(pool, r):
            for k in range(NC):
                if k in r.slots:
                    two = parity2(r, k)
                    _, n = cell_cols(CELLS[k])
                    at_least(pool, gate_done, gate_number(r, k, 1))
                    at_least(pool, c_ready, cell_number(r, k, -2))
                    nc.gpsimd.tensor_tensor(ig[:, two, 0:n], gates[0][two][:, 0:n], gates[1][two][:, 0:n],
                                            ALU.mult).then_inc(ig_ready, 1)
                    if cell_before(r, k):
                        new_h_low(pool, *cell_before(r, k))
                if r.i is None and r.plus < 2:
                    at = EARLY + LATE * (NC * r.plus + k)
                    gather_small(pool, SMALL[at:at + LATE])

        def tanh_of(act, r, k, slot2):
            c, n = c_of(k)
            at_least(act, c_ready, cell_number(r, k))
            nc.scalar.activation(tanh_c[:, slot2, 0:n], c, ACT.Tanh).then_inc(tanh_ready, 1)

        def store_x(act, r, m):
            f, count = SETS[m]
            at, n = f * LANES, count * LANES
            at_least(act, kept_used, units(r, SET_END[m]))
            hx = nwf_hx[r.parity]
            nc.scalar.copy(hx[0][64:128, at:at + n], x_ps[64:128, 0:n])
            nc.scalar.copy(hx[1][0:64, at:at + n], x_ps[0:64, 0:n]).then_inc(nwf_x_done, 1)

        def round_scalar(act, r):
            for k in range(NC):
                kind, par, c = CELLS[k]
                if k in r.slots:
                    two = parity2(r, k)
                    at_least(act, h_low, cell_number(r, k, -2))
                    at_least(act, h_high, cell_number(r, k, -2))
                    at, n = cell_cols(CELLS[k])
                    if r.i is None and r.plus == 1 and k == NWF_SLOTS[0]:
                        act.wait_ge(s_late, 16 * len(late_dmas))
                    for g, (place, func) in enumerate(GATES):
                        at_least(act, gate_ready, gate_number(r, k, g))
                        if kind == "seq":
                            last = nc.scalar.activation(gates[g][two][:, :], g_ps[g][:, :], func)
                        else:
                            for m in cell_sets(c):
                                a, w = SETS[m][0] * LANES - at, SETS[m][1] * LANES
                                last = nc.scalar.activation(gates[g][two][:, a:a + w], g_ps[g][:, a:a + w], func,
                                                            bias=nwf_bias[:, m, place:place + 1])
                        last.then_inc(gate_done, 1)
                    if cell_before(r, k):
                        tanh_of(act, *cell_before(r, k))
                if late_seq_unit(r, k):
                    store_seq_x(act, before(r), late_seq_unit(r, k))
                if k in SEQ_UNIT_SLOTS and r.seq_lookups:
                    store_seq_x(act, r, SEQ_UNIT_SLOTS.index(k))
                for m in range(NSETS):
                    if r.lookups and SET_SLOT[m] == k:
                        store_x(act, r, m)
                    if has_before(r) and SET_SLOT[m] - NC == k:
                        store_x(act, before(r), m)

        def round_tensor(pe, r):
            for k in range(NC):
                kind, par, c = CELLS[k]
                at, n = cell_cols(CELLS[k])
                if k in r.slots:
                    if kind == "seq":
                        back, slot = previous_seq(k)
                        prev = before(r) if back else r
                        at_least(pe, h_low, cell_number(prev, slot))
                        at_least(pe, h_high, cell_number(prev, slot))
                        at_least(pe, seq_x_done, seqs(before(r), SEQ_UNITS.index((par, c // 2))))
                    else:
                        at_least(pe, h_low, cell_number(before(r), k))
                        at_least(pe, h_high, cell_number(before(r), k))
                        at_least(pe, nwf_x_done, sets(before(r), cell_sets(c)[-1]))
                        if r.i is None and r.plus == 1 and c == 0:
                            pe.wait_ge(nwf_w_ready, 4)
                    at_least(pe, gate_done, cell_number(r, k, -1, 4))
                    for g, (place, _) in enumerate(GATES):
                        if kind == "seq":
                            for z in range(2):
                                last = nc.tensor.matmul(g_ps[g][64 * z:64 * z + 64, :], seq_w[:, z, place, :],
                                                        seq_hx[par][z][:, at:at + n], start=True, stop=True)
                        else:
                            for m in cell_sets(c):
                                a, w = SETS[m][0] * LANES, SETS[m][1] * LANES
                                for z in range(2):
                                    last = nc.tensor.matmul(g_ps[g][64 * z:64 * z + 64, a - at:a - at + w],
                                                            nwf_w[:, z, m, place, :],
                                                            nwf_hx[1 - r.parity][z][:, a:a + w],
                                                            start=True, stop=True)
                        last.then_inc(gate_ready, 1)
                if late_seq_unit(r, k):
                    seq_products(pe, before(r), late_seq_unit(r, k))
                if k in SEQ_UNIT_SLOTS and r.seq_lookups:
                    seq_products(pe, r, SEQ_UNIT_SLOTS.index(k))
                for prev, u in ([(r, 2 * k - 2), (r, 2 * k - 1)] if k and r.lookups else
                                [(before(r), NU - 2), (before(r), NU - 1)] if not k and has_before(r) else []):
                    bring(pe, prev, u)
                if r.lookups:
                    for u in (2 * k, 2 * k + 1):
                        ty, m, _ = UNITS[u]
                        slot = unit_of(r, u)
                        at_least(pe, onehot_ready, units(r, u))
                        at_least(pe, kept_ready, units(r, u, -2))
                        for part in range(3):
                            for g in range(4):
                                last = nc.tensor.matmul(e_ps[u % 2][32 * g:32 * g + 32, :], tab[:, part, 2 * m + ty, :],
                                                        onehot[:, slot, g * CH:(g + 1) * CH],
                                                        start=(part == 0), stop=(part == 2))
                        last.then_inc(looked_up, 1)

        def bring(pe, r, u):
            ty, m, quads = UNITS[u]
            n = SETS[m][1] * LANES
            at_least(pe, kept_ready, units(r, u))
            if ty == 0 and quads[0] == 0:
                at_least(pe, nwf_x_done, sets(r, m, -1))
            for i, q in enumerate(quads):
                last = nc.tensor.matmul(x_ps[QUAD_AT[q]:QUAD_AT[q] + 32, 0:n],
                                        cst[:, C_RED + 32 * ty:C_RED + 32 * ty + 32],
                                        kept[:, unit_of(r, u), i * n:(i + 1) * n], start=(ty == 0), stop=(ty == 1))
            last.then_inc(kept_used, 1)

        def regroup_small(sp):
            sp.wait_ge(small_ready, 1)
            for s in range(4):
                sp.dma_start(rest[FEATURES * NWF_H:REST, s::4, :],
                             small[32 * s:32 * s + SMALL_DIMS, :].rearrange("d (q b) -> d q b", q=4)
                             ).then_inc(rest_here, 16)

        def regroup_h(queue, c):
            at, n = NWF_CELLS[c]
            for done in (h_low, h_high):
                queue.wait_ge(done, cell_number(TAIL[-1], NWF_SLOTS[c]))
            for z in range(2):
                queue.dma_start(h_dram[8 * z:8 * z + 8, :, at:at + n].rearrange("s u c -> (s u) c"),
                                nwf_hx[0][z][64 * z:64 * z + 64, at:at + n]).then_inc(h_in_dram[c], 16)
            queue.wait_ge(h_in_dram[c], 32)
            for j in range(at // LANES, (at + n) // LANES):
                queue.dma_start(rest[NWF_H * j:NWF_H * j + NWF_H, :, :],
                                h_dram[:, :, j * LANES:(j + 1) * LANES].rearrange("s u b -> u s b")
                                ).then_inc(rest_here, 16)

        def dense(pe):
            y_ps = [e_ps[z][:, :].rearrange("b (s o) -> b s o", s=8) for z in range(2)]
            pe.wait_ge(s_late, 16 * len(late_dmas))
            for done in (h_low, h_high):
                pe.wait_ge(done, cell_number(TAIL[-2], SEQ_SLOTS[-1]))
            for s in range(SLOTS):
                for half in range(2):
                    nc.tensor.matmul(y_ps[s // 8][:, s % 8, :], seq_hx[0][half][:, s * LANES:(s + 1) * LANES],
                                     seq_out_w[:, half, :], start=(half == 0 and s % 8 == 0), stop=False,
                                     skip_group_check=True)
            pe.wait_ge(rest_here, 16 * (4 + FEATURES))
            for s in range(SLOTS):
                last = nc.tensor.matmul(y_ps[s // 8][:, s % 8, :], rest[:, s, :], rest_w[:, :],
                                        start=False, stop=(s % 8 == 7), skip_group_check=True)
                if s % 8 == 7:
                    last.then_inc(y_summed, 1)

        PAIRS = (NWF_T - 4) // 2
        HEAD = [Round(None, 0, n) for n in range(2)]
        TAIL = [Round(None, 0, n) for n in range(NWF_T - 2, NWF_T + 1)]

        with nc.Block() as block:
            @block.sync
            def _(sp):
                for r in HEAD:
                    round_sync(sp, r, r.plus, 2 * r.plus + 2)
                with sp.Fori(0, PAIRS) as i:
                    for h in range(2, 4):
                        round_sync(sp, Round(i, 2, h), i * 2 + h, i * 4 + (2 * h + 2))
                for r in TAIL[:-1]:
                    round_sync(sp, r, r.plus, 2 * r.plus + 2)
                regroup_small(sp)
                for c in range(2):
                    regroup_h(sp, c)
                for z in range(2):
                    sp.wait_ge(y_ready, z + 1)
                    sp.dma_start(out.rearrange("(b s) o -> b s o", s=SLOTS)[:, 8 * z:8 * z + 8, :],
                                 y[:, 8 * z:8 * z + 8, :]).then_inc(y_stored, 16)
                sp.wait_ge(y_stored, 32)

            @block.vector
            def _(dve):
                for r in HEAD:
                    round_vector(dve, r)
                with dve.Fori(0, PAIRS) as i:
                    for h in range(2, 4):
                        round_vector(dve, Round(i, 2, h))
                for r in TAIL:
                    round_vector(dve, r)
                new_h_high(dve, TAIL[-1], NC - 1, parity2(TAIL[-1], NC - 1))
                for z in range(2):
                    dve.wait_ge(y_summed, z + 1)
                    nc.vector.tensor_scalar(y[:, 8 * z:8 * z + 8, :].rearrange("b s o -> b (s o)"), e_ps[z][:, :],
                                            0.0, None, ALU.max).then_inc(y_ready, 1)

            @block.gpsimd
            def _(pool):
                for r in HEAD:
                    round_gpsimd(pool, r)
                with pool.Fori(0, PAIRS) as i:
                    for h in range(2, 4):
                        round_gpsimd(pool, Round(i, 2, h))
                for r in TAIL:
                    round_gpsimd(pool, r)
                new_h_low(pool, TAIL[-1], NC - 1, parity2(TAIL[-1], NC - 1))

            @block.scalar
            def _(act):
                for r in HEAD:
                    round_scalar(act, r)
                with act.Fori(0, PAIRS) as i:
                    for h in range(2, 4):
                        round_scalar(act, Round(i, 2, h))
                for r in TAIL[:-1]:
                    round_scalar(act, r)
                act.wait_ge(small_turned, 1)
                nc.scalar.copy(small[:, :], sx_ps[:, :]).then_inc(small_ready, 1)
                round_scalar(act, TAIL[-1])
                tanh_of(act, TAIL[-1], NC - 1, parity2(TAIL[-1], NC - 1))
                regroup_h(act, 2)

            @block.tensor
            def _(pe):
                for r in HEAD:
                    round_tensor(pe, r)
                with pe.Fori(0, PAIRS) as i:
                    for h in range(2, 4):
                        round_tensor(pe, Round(i, 2, h))
                for r in TAIL[:-1]:
                    round_tensor(pe, r)
                pe.wait_ge(s_gather, 16 * len(SMALL))
                rows = small_rows[:, :, :].rearrange("b s d -> b (s d)")
                for q in range(4):
                    last = nc.tensor.transpose(sx_ps[:, q * LANES:(q + 1) * LANES], rows[:, q * P:(q + 1) * P],
                                               cst[:, C_ID:C_ID + P])
                last.then_inc(small_turned, 1)
                round_tensor(pe, TAIL[-1])
                dense(pe)

        work.close()


def constants():
    c = np.zeros((P, C_ALL), np.float32)
    c[:, C_ID:C_ID + P] = np.eye(P, dtype=np.float32)
    p = np.arange(P)
    quarter, high, dim = p // 32, (p % 32) // 4, p % 4
    for ty in range(2):
        c[p, C_RED + 32 * ty + 8 * quarter + 4 * ty + dim] = 1.0
    c[:, C_DIAG:C_DIAG + 64] = (p[:, None] % 64) // 8 == np.arange(64)[None, :] // 8
    c[:, C_LOW] = LOW_BASE + p
    part = (VOCAB, P - VOCAB, 2 * VOCAB - P)
    c[:, C_SEQ] = np.where(p < part[0], p, p - part[0])
    c[:, C_SEQ + 1] = np.where(p < part[2], p + part[1], np.where(p < part[2] + VOCAB, p - part[2], -1))
    for n, rows in enumerate((part[0], part[2])):
        c[:, C_FIRST + 2 * n] = p < rows
        c[:, C_FIRST + 2 * n + 1] = p >= rows
    c[:, C_HIGH] = HIGH_BASE * 2.0 ** high
    return c


_INS = ["r_goby_idx", "r_is_indel", "r_matches_ref", "r_from_seq", "r_to_seq", "r_count_fwd", "r_count_rev",
        "r_nwf_numbers", "r_nwf_freqs", "L0_rec_goby_emb", "L0_rec_bool_emb", "L0_rec_count_emb",
        "L0_rec_base_emb", "L0_rec_seq_Wx", "L0_rec_seq_Wh", "L0_rec_seq_b", "L0_rec_nwf_num_emb",
        "L0_rec_nwf_freq_emb", "L0_rec_nwf_Wx", "L0_rec_nwf_Wh", "L0_rec_nwf_b", "L0_rec_reduce_W",
        "L0_rec_reduce_b"]


def kernel(**inputs):
    import concourse.bacc as bacc
    from concourse.bass_utils import run_bass_kernel_spmd

    nc = bacc.Bacc("TRN2", target_bir_lowering=False, num_devices=1)
    arrays, args = {}, []
    for name in _INS:
        a = np.ascontiguousarray(inputs[name])
        arrays[f"in_{name}"] = a
        args.append(nc.dram_tensor(f"in_{name}", a.shape, mybir.dt.from_np(a.dtype), kind="ExternalInput").ap())
    c = constants()
    arrays["in_consts"] = c
    args.append(nc.dram_tensor("in_consts", c.shape, F32, kind="ExternalInput").ap())
    args.append(nc.dram_tensor("out_y", (B, OUT), F32, kind="ExternalOutput").ap())
    build(nc, *args)
    r = run_bass_kernel_spmd(nc, [arrays], core_ids=[0])
    return r.results[0]["out_y"]
```
